# Optimizing a Trainium2 kernel written in Bass

```python
import numpy as np
import jax
import jax.numpy as jnp

def _softmax(x, axis=-1):
    return jax.nn.softmax(x, axis=axis)

def _gelu(x):
    return jax.nn.gelu(x, approximate=True)

def _silu(x):
    return jax.nn.silu(x)

def _sigmoid(x):
    return jax.nn.sigmoid(x)

def _layernorm(x, axis=-1, eps=1e-05):
    m = jnp.mean(x, axis=axis, keepdims=True)
    v = jnp.var(x, axis=axis, keepdims=True)
    return (x - m) / jnp.sqrt(v + eps)

def _scatter_add(tgt, idx, src, axis=0):
    return tgt.at[idx].add(src)

def _segment_sum(src, seg, n):
    return jax.ops.segment_sum(src, seg, n)
kernel_name = 'mk_xattn_ffn_d1_seqx_r4_76f07a'

def setup_inputs(seed: int=0):
    np.random.seed(seed)
    _w = jnp.asarray

    def _rec_inputs():
        import jax
        import jax.numpy as jnp
        _rk = jax.random.key(seed)
        x = 7.22e-05 + 1 * jax.random.normal(jax.random.fold_in(_rk, 1), (4, 1024, 256), jnp.float32)
        _lenS = 1024 - jax.random.randint(jax.random.fold_in(_rk, 7), (4,), 0, max(1, 1024 // 4) + 1, jnp.int32)
        _lenS2 = 77 - jax.random.randint(jax.random.fold_in(_rk, 8), (4,), 0, max(1, 77 // 4) + 1, jnp.int32)
        _ctx_1024P = jax.random.normal(jax.random.fold_in(_rk, 11), (4, 16, 256), jnp.float32)
        _ctx_1024c = jax.random.dirichlet(jax.random.fold_in(_rk, 511), 0.3 * jnp.ones((16,), jnp.float32), (4, 77))
        _ctx_1024t = jnp.einsum('bsk,bkd->bsd', _ctx_1024c, _ctx_1024P)
        _ctx_1024t = _ctx_1024t * jax.lax.rsqrt(jnp.mean(jnp.square(_ctx_1024t)) + 1e-12) * 0.953939
        ctx_1024 = 4.13588e-05 + 0.999923 * (_ctx_1024t + 0.3 * jax.random.normal(jax.random.fold_in(_rk, 611), (4, 77, 256), jnp.float32))
        return (x, ctx_1024)
    x, ctx_1024 = _rec_inputs()

    def _L0_xattn_setup():
        import jax, jax.numpy as jnp
        import numpy as np
        H = 16
        D_MODEL = 256
        D_K = D_MODEL // H
        key = jax.random.key(seed)
        ks = jax.random.split(key, 11)
        B, S = (4, 512)
        scale_in = 1.0 / np.sqrt(D_MODEL)
        inp = {'q': jax.random.normal(ks[0], (B, S, D_MODEL), jnp.float32), 'k': jax.random.normal(ks[1], (B, S, D_MODEL), jnp.float32), 'v': jax.random.normal(ks[2], (B, S, D_MODEL), jnp.float32), 'Wq': jax.random.normal(ks[3], (D_MODEL, D_MODEL), jnp.float32) * scale_in, 'bq': jnp.zeros((D_MODEL,), jnp.float32), 'Wk': jax.random.normal(ks[4], (D_MODEL, D_K), jnp.float32) * scale_in, 'bk': jnp.zeros((D_K,), jnp.float32), 'Wv': jax.random.normal(ks[5], (D_MODEL, D_K), jnp.float32) * scale_in, 'bv': jnp.zeros((D_K,), jnp.float32), 'Wo': jax.random.normal(ks[6], (D_MODEL, D_MODEL), jnp.float32) * scale_in, 'bo': jnp.zeros((D_MODEL,), jnp.float32)}
        return inp
    _L0_xattn_all = _L0_xattn_setup()
    _L0_xattn_in = {k: v for k, v in _L0_xattn_all.items() if k in ('Wq', 'bq', 'Wk', 'bk', 'Wv', 'bv', 'Wo', 'bo')}
    del _L0_xattn_all

    def _L0_ffn_setup():
        import jax, jax.numpy as jnp
        import numpy as np
        HIDDEN = 256
        INTER = 1024
        key = jax.random.key(seed)
        k1, k2, k3, k4, k5 = jax.random.split(key, 5)
        hidden_states = jax.random.normal(k1, (4, 512, HIDDEN), dtype=jnp.float32)
        W1 = jax.random.normal(k2, (HIDDEN, INTER), dtype=jnp.float32) * (1.0 / np.sqrt(HIDDEN))
        b1 = jax.random.normal(k3, (INTER,), dtype=jnp.float32) * 0.02
        W2 = jax.random.normal(k4, (INTER, HIDDEN), dtype=jnp.float32) * (1.0 / np.sqrt(INTER))
        b2 = jax.random.normal(k5, (HIDDEN,), dtype=jnp.float32) * 0.02
        return {'hidden_states': hidden_states, 'W1': W1, 'b1': b1, 'W2': W2, 'b2': b2}
    _L0_ffn_all = _L0_ffn_setup()
    _L0_ffn_in = {k: v for k, v in _L0_ffn_all.items() if k in ('W1', 'b1', 'W2', 'b2')}
    del _L0_ffn_all
    return {'x': x, 'ctx_1024': ctx_1024, 'L0_xattn_Wq': _L0_xattn_in['Wq'], 'L0_xattn_bq': _L0_xattn_in['bq'], 'L0_xattn_Wk': _L0_xattn_in['Wk'], 'L0_xattn_bk': _L0_xattn_in['bk'], 'L0_xattn_Wv': _L0_xattn_in['Wv'], 'L0_xattn_bv': _L0_xattn_in['bv'], 'L0_xattn_Wo': _L0_xattn_in['Wo'], 'L0_xattn_bo': _L0_xattn_in['bo'], 'L0_ffn_W1': _L0_ffn_in['W1'], 'L0_ffn_b1': _L0_ffn_in['b1'], 'L0_ffn_W2': _L0_ffn_in['W2'], 'L0_ffn_b2': _L0_ffn_in['b2']}

def reference(x, ctx_1024, L0_xattn_Wq, L0_xattn_bq, L0_xattn_Wk, L0_xattn_bk, L0_xattn_Wv, L0_xattn_bv, L0_xattn_Wo, L0_xattn_bo, L0_ffn_W1, L0_ffn_b1, L0_ffn_W2, L0_ffn_b2):
    import jax
    import jax.numpy as jnp

    def _L0_xattn_ref(q, k, v, Wq, bq, Wk, bk, Wv, bv, Wo, bo):
        import jax, jax.numpy as jnp
        import numpy as np
        H = 16
        D_MODEL = 256
        D_K = D_MODEL // H
        B, S, _ = q.shape
        qh = (q @ Wq + bq).reshape(B, S, H, D_K).transpose(0, 2, 1, 3)
        kh = k @ Wk + bk
        vh = v @ Wv + bv
        scores = jnp.einsum('bhqd,bkd->bhqk', qh, kh) / jnp.sqrt(jnp.float32(D_K))
        p = jax.nn.softmax(scores, axis=-1)
        out = jnp.einsum('bhqk,bkd->bhqd', p, vh)
        out = out.transpose(0, 2, 1, 3).reshape(B, S, H * D_K)
        return out @ Wo + bo

    def _L0_ffn_ref(hidden_states, W1, b1, W2, b2):
        import jax, jax.numpy as jnp
        import numpy as np
        HIDDEN = 256
        INTER = 1024
        h = jax.nn.relu(jnp.einsum('bsh,hi->bsi', hidden_states, W1) + b1)
        return jnp.einsum('bsi,ih->bsh', h, W2) + b2
    x = x + _L0_xattn_ref(_layernorm(x, axis=-1), ctx_1024, ctx_1024, L0_xattn_Wq, L0_xattn_bq, L0_xattn_Wk, L0_xattn_bk, L0_xattn_Wv, L0_xattn_bv, L0_xattn_Wo, L0_xattn_bo)
    x = x + _L0_ffn_ref(_layernorm(x, axis=-1), L0_ffn_W1, L0_ffn_b1, L0_ffn_W2, L0_ffn_b2)
    return x

_drawn_inputs = setup_inputs


def setup_inputs(seed=0):
    import zlib

    import numpy as np

    out = dict(_drawn_inputs(seed))
    spreads = {'L0_xattn_bq': (0.0, 0.326),
     'L0_xattn_bk': (0.0, 0.8),
     'L0_xattn_bv': (0.0, 0.1),
     'L0_xattn_bo': (0.0, 0.1)}
    factors = {'L0_ffn_b1': 5.297, 'L0_ffn_b2': 3.77}
    for name, (base, spread) in spreads.items():
        noise = np.random.default_rng([zlib.crc32(name.encode()), seed]).standard_normal(out[name].shape)
        drawn = base * np.exp(spread * noise) if base else spread * noise
        out[name] = jnp.asarray(drawn.astype(out[name].dtype))
    for name, factor in factors.items():
        out[name] = (out[name] * factor).astype(out[name].dtype)
    return out
```

```python
import concourse.bass as bass
from concourse import mybir
from contextlib import ExitStack

F32 = mybir.dt.float32
F32R = mybir.dt.float32r
ALU = mybir.AluOpType
ACT = mybir.ActivationFunctionType
AX = mybir.AxisListType

P = 128
NB, SEQ, D = 4, 1024, 256
KEYS = 77
HEADS, DH = 16, 16
FF = 1024
BLK = 512
NT = BLK // P
NBLK = NB * SEQ // BLK
BLK_PER_B = SEQ // BLK
KC = D // P
FC = FF // P
HH = P // DH
HALVES = HEADS // HH
GH = HH // 2
SROW = HH * KEYS
GROW = GH * KEYS
PC = -(-SROW // P)
PW = PC * P
PAIRS = 3
UNITS = HALVES * NT
SCALE = float(DH) ** -0.5
EPS = 1e-5
HI, LO = 0, 1
PASSES = ((HI, HI), (LO, HI), (HI, LO))


def xattn_ffn(nc, x, ctx, Wq, bq, Wk, bk, Wv, bv, Wo, bo, W1, b1, W2, b2, out):
    x_blk = x.rearrange("b (c t p) d -> (b c) p t d", t=NT, p=P)
    out_blk = out.rearrange("b (c t p) d -> (b c) p t d", t=NT, p=P)
    stack = ExitStack()

    def sb(name, shape, dt=F32):
        return stack.enter_context(nc.sbuf_tensor(name, shape, dt))

    def sem(name):
        return stack.enter_context(nc.semaphore(name))

    def f(ap):
        return ap.bitcast(F32)

    with stack:
        ident = sb("ident", [P, P])
        wq = sb("wq", [P, 2, KC, D], F32R)
        wo = sb("wo", [P, 2, KC, D], F32R)
        w1 = sb("w1", [P, 2, KC, FF], F32R)
        w2 = sb("w2", [P, 2, FC, D], F32R)
        bq_sb = sb("bq_sb", [P, KC])
        b1_sb = sb("b1_sb", [P, FC])
        bk_sb = sb("bk_sb", [P, 1])
        bo_bc = sb("bo_bc", [P, D])
        b2_bc = sb("b2_bc", [P, D])
        bv_bc = sb("bv_bc", [KEYS, DH])
        eps_sb = sb("eps_sb", [P, 1])
        k_rep = sb("k_rep", [P, 2, NB * KEYS])
        v_rows = sb("v_rows", [P, PC, 2, NB, DH])
        k_mask = sb("k_mask", [P, HH])
        v_mask = sb("v_mask", [P, 2, PAIRS, GH])
        k_cur = sb("k_cur", [P, 2, HH, KEYS], F32R)
        v_cur = sb("v_cur", [P, 2, PAIRS, 2, P], F32R)
        x_sb = sb("x_sb", [P, NT, D])
        xb = sb("xb", [P, NT, D])
        xn = sb("xn", [P, NT, D])
        xnT = sb("xnT", [P, 2, KC, BLK], F32R)
        qT = sb("qT", [P, 2, KC, BLK], F32R)
        s_sub = sb("s_sub", [P, 2, PW])
        e_f = sb("e_f", [P, 2, PW])
        pT = sb("pT", [P, 2, HALVES, PC, BLK], F32R)
        att = sb("att", [P, HALVES, BLK])
        attT = sb("attT", [P, 2, HALVES, BLK], F32R)
        smax = sb("smax", [P, 2, HH])
        x2 = sb("x2", [P, NT, D])
        x2b = sb("x2b", [P, NT, D])
        xn2 = sb("xn2", [P, NT, D])
        x2nT = sb("x2nT", [P, 2, KC, BLK], F32R)
        h_f = sb("h_f", [P, 2, BLK])
        st = [sb(f"st{n}", [P, NT, 6]) for n in (1, 2)]
        mv = [sb(f"mv{n}", [P, NT, 2]) for n in (1, 2)]
        nmean = [sb(f"nmean{n}", [P, NT]) for n in (1, 2)]
        lnv = [sb(f"lnv{n}", [P, NT]) for n in (1, 2)]
        rstd = [sb(f"rstd{n}", [P, NT]) for n in (1, 2)]
        with ExitStack() as early:
            def tmp(name, shape):
                return early.enter_context(nc.sbuf_tensor(name, shape, F32))
            w1_raw = tmp("w1_raw", [P, KC, FF])
            w2_raw = tmp("w2_raw", [P, FC, D])
            wo_raw = tmp("wo_raw", [P, KC, D])
            wq_raw = tmp("wq_raw", [P, KC, D])
            ctx_sb = tmp("ctx_sb", [KEYS, NB, D])
            ctxT = tmp("ctxT", [P, KC, NB * KEYS])
            wk_raw = tmp("wk_raw", [P, KC, DH])
            wk_rep = tmp("wk_rep", [P, KC, HH, DH])
            wv_sb = tmp("wv_sb", [P, KC, DH])
            v_f = tmp("v_f", [KEYS, NB, DH])
            v_all = tmp("v_all", [KEYS, 2, NB, DH])
        hT = sb("hT", [P, 2, FC, BLK], F32R)
        sel = x2b[0:KEYS, :, :].rearrange("k t d -> k (t d)")[:, 0:PW]

        s_ps = stack.enter_context(nc.psum_tensor("s_ps", [P, 4, 512], F32))
        t_ps = stack.enter_context(nc.psum_tensor("t_ps", [P, 2, 512], F32))
        g_ps = stack.enter_context(nc.psum_tensor("g_ps", [P, 2, 512], F32))
        t_flat = t_ps[:, :, :].rearrange("p a b -> p (a b)")

        kv_loaded, wk_loaded = sem("kv_loaded"), sem("wk_loaded")
        bias_loaded, wq_loaded, wo_loaded = sem("bias_loaded"), sem("wq_loaded"), sem("wo_loaded")
        w1_loaded, w2_loaded = sem("w1_loaded"), sem("w2_loaded")
        x_loaded, out_stored = sem("x_loaded"), sem("out_stored")
        setup_pool, setup_dve, setup_act, setup_pe = (sem(f"setup_{e}") for e in ("pool", "dve", "act", "pe"))
        w_hi, w_lo = sem("w_hi"), sem("w_lo")
        stats_done = [sem(f"stats{n}_done") for n in (1, 2)]
        aggr_done = [sem(f"aggr{n}_done") for n in (1, 2)]
        nmean_done = [sem(f"nmean{n}_done") for n in (1, 2)]
        lnv_done = [sem(f"lnv{n}_done") for n in (1, 2)]
        rstd_done = [sem(f"rstd{n}_done") for n in (1, 2)]
        xn_done, xn2_done = sem("xn_done"), sem("xn2_done")
        xb_done, x2b_done = sem("xb_done"), sem("x2b_done")
        xnT_ps, xnT_hi, xnT_lo = sem("xnT_ps"), sem("xnT_hi"), sem("xnT_lo")
        q_ps, q_hi, q_lo = sem("q_ps"), sem("q_hi"), sem("q_lo")
        k_ready, v_ready = sem("k_ready"), sem("v_ready")
        score_ps, max_done, sub_done = sem("score_ps"), sem("max_done"), sem("sub_done")
        subT_ps, p_hi, e_done, p_lo = sem("subT_ps"), sem("p_hi"), sem("e_done"), sem("p_lo")
        pv_ps, log_done, inv_done, att_done = sem("pv_ps"), sem("log_done"), sem("inv_done"), sem("att_done")
        att_hi, att_lo = sem("att_hi"), sem("att_lo")
        o_ps, x2_done = sem("o_ps"), sem("x2_done")
        x2nT_ps, x2nT_hi, x2nT_lo = sem("x2nT_ps"), sem("x2nT_hi"), sem("x2nT_lo")
        h_ps, h_hi, hf_done, h_lo = sem("h_ps"), sem("h_hi"), sem("hf_done"), sem("h_lo")
        y_ps, out_done = sem("y_ps"), sem("out_done")

        block = stack.enter_context(nc.Block())

        w1_pieces = [(w1_raw[:, c, h * 512:(h + 1) * 512], w1[:, HI, c, h * 512:(h + 1) * 512],
                      w1[:, LO, c, h * 512:(h + 1) * 512], w1_loaded) for c in range(KC) for h in range(2)]
        w2_pieces = [(w2_raw[:, c:c + 2, :], w2[:, HI, c:c + 2, :], w2[:, LO, c:c + 2, :], w2_loaded)
                     for c in range(0, FC, 2)]
        pieces = w1_pieces + w2_pieces
        assert len(pieces) == UNITS

        def group_part(g):
            a = (g % 2) * 64
            return slice(a, a + 64), slice(64 - a, 128 - a)

        @block.sync
        def _(eng):
            eng.dma_start(x_sb[:, :, :], x_blk[0]).then_inc(x_loaded, 16)
            eng.dma_start(wq_raw[:, :, :], Wq.rearrange("(c p) n -> p c n", p=P)).then_inc(wq_loaded, 16)
            eng.dma_start(wo_raw[:, :, :], Wo.rearrange("(c p) n -> p c n", p=P)).then_inc(wo_loaded, 16)
            eng.dma_start(w1_raw[:, :, :], W1.rearrange("(c p) n -> p c n", p=P)).then_inc(w1_loaded, 16)
            eng.dma_start(w2_raw[:, :, :], W2.rearrange("(c p) n -> p c n", p=P)).then_inc(w2_loaded, 16)

            def load_next(i):
                eng.wait_ge(xb_done, i + 1)
                eng.dma_start(x_sb[:, :, :], x_blk[i + 1]).then_inc(x_loaded, 16)

            def store(i):
                for tp in range(2):
                    eng.wait_ge(out_done, 2 * i + tp + 1)
                    eng.dma_start(out_blk[i][:, 2 * tp:2 * tp + 2, :],
                                  x2b[:, 2 * tp:2 * tp + 2, :]).then_inc(out_stored, 16)

            load_next(0)
            load_next(1)
            store(0)
            with eng.Fori(2, NBLK - 1) as i:
                load_next(i)
                store(i - 1)
            store(NBLK - 2)
            store(NBLK - 1)
            eng.wait_ge(out_stored, 32 * NBLK)

        @block.tensor
        def _(eng):
            def mm3(o, lhs, rhs, steps):
                n = len(steps) * len(PASSES)
                j = 0
                for s in steps:
                    for a, b in PASSES:
                        last = nc.tensor.matmul(o, lhs(a, s), rhs(b, s), start=(j == 0), stop=(j == n - 1))
                        j += 1
                return last

            def transpose_rows(src, done):
                for c in range(KC):
                    for t in range(NT):
                        last = nc.tensor.transpose(t_ps[:, c, t * P:(t + 1) * P],
                                                   src[:, t, c * P:(c + 1) * P], ident[:, :])
                    last.then_inc(done, 1)

            def queries():
                for m in range(KC):
                    mm3(s_ps[:, m, :], lambda a, c: wq[:, a, c, m * P:(m + 1) * P],
                        lambda b, c: xnT[:, b, c, :], range(KC)).then_inc(q_ps, 1)

            def scores(u):
                hf, t = divmod(u, NT)
                for j in range(2):
                    last = mm3(s_ps[:, 2 * (u % 2) + j, 0:GROW],
                               lambda a, c: qT[:, a, hf, t * P:(t + 1) * P],
                               lambda b, c: k_cur[:, b, j * GH:(j + 1) * GH, :].rearrange("p h k -> p (h k)"),
                               [0])
                last.then_inc(score_ps, 1)

            def ffn_in(k):
                mm3(g_ps[:, k % 2, :], lambda a, c: w1[:, a, c, k * P:(k + 1) * P],
                    lambda b, c: x2nT[:, b, c, :], range(KC)).then_inc(h_ps, 1)

            def ffn_out(tp):
                for t in (2 * tp, 2 * tp + 1):
                    last = mm3(g_ps[:, tp, (t % 2) * D:(t % 2 + 1) * D],
                               lambda a, k: hT[:, a, k, t * P:(t + 1) * P],
                               lambda b, k: w2[:, b, k, :], range(FC))
                last.then_inc(y_ps, 1)

            def step(i, ffn, more):
                if ffn:
                    eng.wait_ge(x2nT_lo, 2 * i)
                for k in range(UNITS):
                    if ffn:
                        if k >= 2:
                            eng.wait_ge(hf_done, 8 * (i - 1) + k - 1)
                        ffn_in(k)
                    eng.wait_ge(sub_done, 8 * i + k + 1)
                    if k >= 1:
                        eng.wait_ge(e_done, 8 * i + k)
                    for c in range(PC):
                        last = nc.tensor.transpose(t_flat[:, c * P:(c + 1) * P],
                                                   s_sub[:, k % 2, c * P:(c + 1) * P], ident[:, :])
                    last.then_inc(subT_ps, 1)
                    if k + 2 < UNITS:
                        scores(k + 2)
                eng.wait_ge(v_ready, i + 1)
                for g in range(4):
                    hf, gg = divmod(g, 2)
                    if gg == 0:
                        eng.wait_ge(p_lo, 8 * i + NT * (hf + 1))
                    mm3(s_ps[:, g, :], lambda a, j: v_cur[:, gg, j, a, :],
                        lambda b, j: pT[:, b, hf, 2 * gg + j, :], range(PAIRS)).then_inc(pv_ps, 1)
                if more:
                    eng.wait_ge(xn_done, 4 * (i + 2))
                    transpose_rows(xn, xnT_ps)
                if ffn:
                    eng.wait_ge(h_lo, 8 * i)
                    ffn_out(0)
                if not ffn:
                    eng.wait_ge(w_lo, 1)
                if more:
                    eng.wait_ge(xnT_lo, 2 * (i + 2))
                eng.wait_ge(att_lo, 2 * (i + 1))
                for tp in range(2):
                    for t in (2 * tp, 2 * tp + 1):
                        last = mm3(t_ps[:, tp, (t % 2) * D:(t % 2 + 1) * D],
                                   lambda a, c: attT[:, a, c, t * P:(t + 1) * P],
                                   lambda b, c: wo[:, b, c, :], range(KC))
                    last.then_inc(o_ps, 1)
                if more:
                    queries()
                if ffn:
                    ffn_out(1)
                eng.wait_ge(xn2_done, 4 * (i + 1))
                transpose_rows(xn2, x2nT_ps)
                if more:
                    eng.wait_ge(q_lo, 2 * (i + 2))
                    eng.wait_ge(k_ready, i + 2)
                    scores(0)
                    scores(1)

            eng.wait_ge(setup_pool, 2)
            eng.wait_ge(kv_loaded, 16)
            for c in range(KC):
                for b in range(NB):
                    last = nc.tensor.transpose(s_ps[:, c, b * KEYS:(b + 1) * KEYS],
                                               ctx_sb[:, b, c * P:(c + 1) * P], ident[0:KEYS, 0:KEYS])
            last.then_inc(setup_pe, 1)
            eng.wait_ge(setup_act, 1)
            eng.wait_ge(setup_dve, 2)
            for c in range(KC):
                last = nc.tensor.matmul(s_ps[:, 2, 0:NB * KEYS], wk_rep[:, c, :, :].rearrange("p h d -> p (h d)"),
                                        ctxT[:, c, :], start=(c == 0), stop=(c == KC - 1))
            last.then_inc(setup_pe, 1)
            for b in range(NB):
                for c in range(KC):
                    last = nc.tensor.matmul(s_ps[0:KEYS, 3, b * DH:(b + 1) * DH],
                                            ctxT[:, c, b * KEYS:(b + 1) * KEYS], wv_sb[:, c, :],
                                            start=(c == 0), stop=(c == KC - 1))
            last.then_inc(setup_pe, 1)
            eng.wait_ge(xn_done, 4)
            transpose_rows(xn, xnT_ps)
            eng.wait_ge(setup_dve, 5)
            eng.wait_ge(setup_pool, 4)
            for c in range(PC):
                last = nc.tensor.matmul(g_ps[:, c // 4, (c % 4) * P:(c % 4 + 1) * P],
                                        sel[:, c * P:(c + 1) * P],
                                        v_all[:, :, :, :].rearrange("k a b d -> k (a b d)"),
                                        start=True, stop=True)
            last.then_inc(setup_pe, 1)
            eng.wait_ge(xnT_lo, 2)
            eng.wait_ge(w_lo, 2)
            queries()
            eng.wait_ge(q_lo, 2)
            eng.wait_ge(k_ready, 1)
            scores(0)
            scores(1)

            step(0, False, True)
            step(1, True, True)
            with eng.Fori(2, NBLK - 1) as i:
                step(i, True, True)
            step(NBLK - 1, True, False)
            eng.wait_ge(x2nT_lo, 2 * NBLK)
            for k in range(FC):
                if k >= 2:
                    eng.wait_ge(hf_done, 8 * (NBLK - 1) + k - 1)
                ffn_in(k)
            eng.wait_ge(h_lo, 8 * NBLK)
            ffn_out(0)
            ffn_out(1)

        @block.scalar
        def _(eng):
            eng.dma_start(ctx_sb[:, :, :], ctx.rearrange("b k d -> k b d")).then_inc(kv_loaded, 16)
            eng.dma_start(wk_raw[:, :, :], Wk.rearrange("(c p) n -> p c n", p=P)).then_inc(wk_loaded, 16)
            eng.dma_start(wv_sb[:, :, :], Wv.rearrange("(c p) n -> p c n", p=P)).then_inc(wk_loaded, 16)
            for h in range(HH):
                eng.dma_start(bk_sb[h * DH:(h + 1) * DH, :], bk.rearrange("(d a) -> d a", a=1)).then_inc(bias_loaded, 16)
            eng.dma_start(bq_sb[:, :], bq.rearrange("(m p) -> p m", p=P), allow_slow_non_contiguous=True).then_inc(bias_loaded, 16)
            eng.dma_start(b1_sb[:, :], b1.rearrange("(m p) -> p m", p=P), allow_slow_non_contiguous=True).then_inc(bias_loaded, 16)
            eng.dma_start(bv_bc[:, :], bv.partition_broadcast(KEYS)).then_inc(bias_loaded, 16)
            eng.dma_start(bo_bc[:, :], bo.partition_broadcast(P)).then_inc(bias_loaded, 16)
            eng.dma_start(b2_bc[:, :], b2.partition_broadcast(P)).then_inc(bias_loaded, 16)

            def inv_std(n, i):
                eng.wait_ge(nmean_done[n], i + 1)
                nc.scalar.activation(lnv[n][:, :], mv[n][:, :, 1], ACT.Ln, bias=eps_sb[:, :]).then_inc(lnv_done[n], 1)
                eng.wait_ge(lnv_done[n], i + 1)
                nc.scalar.activation(rstd[n][:, :], lnv[n][:, :], ACT.Exp, scale=-0.5).then_inc(rstd_done[n], 1)

            def rows_high(dst, ps_done, done, i):
                for c in range(KC):
                    eng.wait_ge(ps_done, 2 * i + c + 1)
                    nc.scalar.activation(dst[:, HI, c, :], t_ps[:, c, :], ACT.Copy).then_inc(done, 1)

            def query_high(i, m):
                eng.wait_ge(q_ps, 2 * i + m + 1)
                nc.scalar.activation(qT[:, HI, m, :], s_ps[:, m, :], ACT.Identity,
                                     bias=bq_sb[:, m:m + 1]).then_inc(q_hi, 1)

            def hidden(i, k):
                eng.wait_ge(h_ps, 8 * i + k + 1)
                nc.scalar.activation(hT[:, HI, k, :], g_ps[:, k % 2, :], ACT.Relu,
                                     bias=b1_sb[:, k:k + 1]).then_inc(h_hi, 1)
                if k >= 2:
                    eng.wait_ge(h_lo, 8 * i + k - 1)
                nc.scalar.activation(h_f[:, k % 2, :], g_ps[:, k % 2, :], ACT.Relu,
                                     bias=b1_sb[:, k:k + 1]).then_inc(hf_done, 1)

            def step(i, ffn, more):
                for k in range(UNITS):
                    if ffn:
                        hidden(i - 1, k)
                    hf, t = divmod(k, NT)
                    eng.wait_ge(subT_ps, 8 * i + k + 1)
                    src = t_flat[:, 0:PW].rearrange("p (c t) -> p c t", t=P)
                    nc.scalar.activation(pT[:, HI, hf, :, t * P:(t + 1) * P], src, ACT.Exp,
                                         scale=SCALE).then_inc(p_hi, 1)
                    if k >= 2:
                        eng.wait_ge(p_lo, 8 * i + k - 1)
                    nc.scalar.activation(e_f[:, k % 2, :], t_flat[:, 0:PW], ACT.Exp,
                                         scale=SCALE).then_inc(e_done, 1)
                    if not ffn:
                        raw, high, _, loaded = pieces[k]
                        eng.wait_ge(loaded, 16)
                        nc.scalar.activation(high, raw, ACT.Copy).then_inc(w_hi, 1)
                for g in range(4):
                    num, den = group_part(g)
                    hf = g // 2
                    if g == 1 and more:
                        inv_std(0, i + 1)
                    eng.wait_ge(pv_ps, 4 * i + g + 1)
                    nc.scalar.activation(att[num, hf, :], s_ps[den, g, :], ACT.Ln).then_inc(log_done, 1)
                    eng.wait_ge(log_done, 4 * i + g + 1)
                    nc.scalar.activation(att[num, hf, :], att[num, hf, :], ACT.Exp, scale=-1.0).then_inc(inv_done, 1)
                    if g == 2:
                        att_high(i, 0)
                if more:
                    rows_high(xnT, xnT_ps, xnT_hi, i + 1)
                att_high(i, 1)
                if more:
                    query_high(i + 1, 0)
                    inv_std(1, i)
                    query_high(i + 1, 1)
                else:
                    inv_std(1, i)
                rows_high(x2nT, x2nT_ps, x2nT_hi, i)

            def att_high(i, hf):
                eng.wait_ge(att_done, 4 * i + 2 * hf + 2)
                nc.scalar.activation(attT[:, HI, hf, :], att[:, hf, :], ACT.Copy).then_inc(att_hi, 1)

            eng.preload_act_table_set("natural_log_exp_and_others")
            eng.wait_ge(setup_pe, 1)
            nc.scalar.activation(ctxT[:, :, :], s_ps[:, 0:KC, 0:NB * KEYS], ACT.Copy).then_inc(setup_act, 1)
            eng.wait_ge(setup_dve, 2)
            inv_std(0, 0)
            eng.wait_ge(bias_loaded, 16 * (HH + 5))
            eng.wait_ge(setup_pe, 2)
            nc.scalar.activation(k_rep[:, HI, :].bitcast(F32R), s_ps[:, 2, 0:NB * KEYS], ACT.Identity,
                                 bias=bk_sb[:, :]).then_inc(setup_act, 1)
            rows_high(xnT, xnT_ps, xnT_hi, 0)
            for raw, high, loaded in ((wo_raw, wo, wo_loaded), (wq_raw, wq, wq_loaded)):
                eng.wait_ge(loaded, 16)
                nc.scalar.activation(high[:, HI, :, :], raw[:, :, :], ACT.Copy).then_inc(w_hi, 1)
            query_high(0, 0)
            query_high(0, 1)

            step(0, False, True)
            step(1, True, True)
            with eng.Fori(2, NBLK - 1) as i:
                step(i, True, True)
            step(NBLK - 1, True, False)
            for k in range(FC):
                hidden(NBLK - 1, k)

        @block.vector
        def _(eng):
            def stats(n, src, i, tiles):
                for t in tiles:
                    nc.vector.bn_stats(st[n][:, t, :], src[:, t, :]).then_inc(stats_done[n], 1)

            def moments(n, i):
                for t in range(NT):
                    nc.vector.bn_aggr(mv[n][:, t, :], st[n][:, t, :]).then_inc(aggr_done[n], 1)
                eng.wait_ge(aggr_done[n], 4 * (i + 1))
                nc.vector.tensor_scalar(nmean[n][:, :], mv[n][:, :, 0], -1.0, None, ALU.mult).then_inc(nmean_done[n], 1)

            def rows_low(dst, high_done, done, i):
                for c in range(KC):
                    eng.wait_ge(high_done, 2 * i + c + 1)
                    nc.vector.tensor_tensor(dst[:, LO, c, :], t_ps[:, c, :], f(dst[:, HI, c, :]),
                                            ALU.subtract).then_inc(done, 1)

            def query_low(i, m):
                eng.wait_ge(q_hi, 2 * i + m + 1)
                nc.vector.scalar_tensor_tensor(qT[:, LO, m, :], s_ps[:, m, :], bq_sb[:, m:m + 1],
                                               f(qT[:, HI, m, :]), ALU.add, ALU.subtract).then_inc(q_lo, 1)

            def prob_low(i, k):
                hf, t = divmod(k, NT)
                eng.wait_ge(e_done, 8 * i + k + 1)
                nc.vector.tensor_tensor(pT[:, LO, hf, :, t * P:(t + 1) * P],
                                        e_f[:, k % 2, :].rearrange("p (c t) -> p c t", t=P),
                                        f(pT[:, HI, hf, :, t * P:(t + 1) * P]), ALU.subtract).then_inc(p_lo, 1)

            def att_low(i, hf):
                eng.wait_ge(att_hi, 2 * i + hf + 1)
                nc.vector.tensor_tensor(attT[:, LO, hf, :], att[:, hf, :], f(attT[:, HI, hf, :]),
                                        ALU.subtract).then_inc(att_lo, 1)

            def result(i, tp):
                eng.wait_ge(y_ps, 2 * i + tp + 1)
                nc.vector.tensor_tensor(x2b[:, 2 * tp:2 * tp + 2, :],
                                        g_ps[:, tp, :].rearrange("p (t d) -> p t d", d=D),
                                        x2b[:, 2 * tp:2 * tp + 2, :], ALU.add).then_inc(out_done, 1)

            def step(i, ffn, more):
                for k in range(UNITS):
                    eng.wait_ge(score_ps, 8 * i + k + 1)
                    s = s_ps[:, 2 * (k % 2):2 * (k % 2) + 2, 0:GROW].rearrange("p j (h k) -> p j h k", k=KEYS)
                    m = smax[:, k % 2, :].rearrange("p (j h) -> p j h", j=2)
                    nc.vector.tensor_reduce(m, s, AX.X, ALU.max).then_inc(max_done, 1)
                    if k >= 2:
                        prob_low(i, k - 2)
                        eng.wait_ge(subT_ps, 8 * i + k - 1)
                    eng.wait_ge(max_done, 8 * i + k + 1)
                    nc.vector.tensor_tensor(s_sub[:, k % 2, 0:SROW].rearrange("p (j h k) -> p j h k", j=2, k=KEYS),
                                            s, m.unsqueeze(3).broadcast_to([P, 2, GH, KEYS]),
                                            ALU.subtract).then_inc(sub_done, 1)
                    if not ffn:
                        raw, high, low, _ = pieces[k]
                        eng.wait_ge(w_hi, 2 + k + 1)
                        nc.vector.tensor_tensor(low, raw, f(high), ALU.subtract).then_inc(w_lo, 1)
                prob_low(i, UNITS - 2)
                prob_low(i, UNITS - 1)
                if more:
                    eng.wait_ge(x_loaded, 16 * (i + 2))
                    stats(0, x_sb, i + 1, range(NT))
                    eng.wait_ge(stats_done[0], 4 * (i + 2))
                for g in range(4):
                    num, _ = group_part(g)
                    if g == 1 and more:
                        moments(0, i + 1)
                    eng.wait_ge(inv_done, 4 * i + g + 1)
                    nc.vector.tensor_tensor(att[num, g // 2, :], s_ps[num, g, :], att[num, g // 2, :],
                                            ALU.mult).then_inc(att_done, 1)
                    if g == 2:
                        att_low(i, 0)
                if more:
                    rows_low(xnT, xnT_hi, xnT_lo, i + 1)
                att_low(i, 1)
                if ffn:
                    result(i - 1, 0)
                    eng.wait_ge(x2b_done, i)
                for tp in range(2):
                    eng.wait_ge(o_ps, 2 * i + tp + 1)
                    nc.vector.tensor_tensor(x2[:, 2 * tp:2 * tp + 2, :],
                                            t_ps[:, tp, :].rearrange("p (t d) -> p t d", d=D),
                                            xb[:, 2 * tp:2 * tp + 2, :], ALU.add).then_inc(x2_done, 1)
                for tp in range(2):
                    eng.wait_ge(x2_done, 2 * i + tp + 1)
                    stats(1, x2, i, (2 * tp, 2 * tp + 1))
                eng.wait_ge(stats_done[1], 4 * (i + 1))
                if more:
                    query_low(i + 1, 0)
                moments(1, i)
                if more:
                    query_low(i + 1, 1)
                if ffn:
                    result(i - 1, 1)
                rows_low(x2nT, x2nT_hi, x2nT_lo, i)

            nc.vector.memset(eps_sb[:, :], EPS)
            nc.vector.memset(s_sub[:, :, SROW:PW], 0.0).then_inc(setup_dve, 1)
            eng.wait_ge(wk_loaded, 32)
            nc.vector.tensor_copy(wk_rep[:, :, :, :],
                                  wk_raw[:, :, :].unsqueeze(2).broadcast_to([P, KC, HH, DH])).then_inc(setup_dve, 1)
            eng.wait_ge(x_loaded, 16)
            stats(0, x_sb, 0, range(NT))
            eng.wait_ge(stats_done[0], 4)
            moments(0, 0)
            eng.wait_ge(bias_loaded, 16 * (HH + 5))
            eng.wait_ge(setup_pe, 3)
            nc.vector.tensor_tensor(v_f[:, :, :], s_ps[0:KEYS, 3, 0:NB * DH].rearrange("k (b d) -> k b d", d=DH),
                                    bv_bc[:, :].unsqueeze(1).broadcast_to([KEYS, NB, DH]), ALU.add).then_inc(setup_dve, 1)
            eng.wait_ge(setup_dve, 3)
            nc.vector.tensor_copy(v_all[:, HI, :, :].bitcast(F32R), v_f[:, :, :]).then_inc(setup_dve, 1)
            eng.wait_ge(setup_dve, 4)
            nc.vector.tensor_tensor(v_all[:, LO, :, :].bitcast(F32R), v_f[:, :, :], v_all[:, HI, :, :],
                                    ALU.subtract).then_inc(setup_dve, 1)
            eng.wait_ge(setup_act, 2)
            nc.vector.scalar_tensor_tensor(k_rep[:, LO, :].bitcast(F32R), s_ps[:, 2, 0:NB * KEYS], bk_sb[:, :],
                                           k_rep[:, HI, :], ALU.add, ALU.subtract).then_inc(setup_dve, 1)
            rows_low(xnT, xnT_hi, xnT_lo, 0)
            for n, (raw, w) in enumerate(((wo_raw, wo), (wq_raw, wq))):
                eng.wait_ge(w_hi, n + 1)
                nc.vector.tensor_tensor(w[:, LO, :, :], raw[:, :, :], f(w[:, HI, :, :]),
                                        ALU.subtract).then_inc(w_lo, 1)
            eng.wait_ge(setup_pe, 4)
            nc.vector.tensor_copy(v_rows[:, 0:4, :, :, :].rearrange("p c a b d -> p (c a b d)"),
                                  g_ps[:, 0, :])
            nc.vector.tensor_copy(v_rows[:, 4, :, :, :].rearrange("p a b d -> p (a b d)"),
                                  g_ps[:, 1, 0:P]).then_inc(setup_dve, 1)
            query_low(0, 0)
            query_low(0, 1)

            step(0, False, True)
            step(1, True, True)
            with eng.Fori(2, NBLK - 1) as i:
                step(i, True, True)
            step(NBLK - 1, True, False)
            result(NBLK - 1, 0)
            result(NBLK - 1, 1)

        @block.gpsimd
        def _(eng):
            def normed(n, dst, src, done):
                for t in range(NT):
                    nc.gpsimd.tensor_scalar(dst[:, t, :], src[:, t, :], nmean[n][:, t:t + 1],
                                            rstd[n][:, t:t + 1], ALU.add, ALU.mult).then_inc(done, 1)

            def plus_row(dst, src, row):
                return nc.gpsimd.tensor_tensor(dst[:, :, :], src[:, :, :],
                                               row[:, :].unsqueeze(1).broadcast_to([P, NT, D]), ALU.add)

            def keys(i):
                b = i // BLK_PER_B
                for a in (HI, LO):
                    last = nc.gpsimd.tensor_tensor(
                        k_cur[:, a, :, :], k_rep[:, a, bass.ds(b * KEYS, KEYS)].unsqueeze(1).broadcast_to([P, HH, KEYS]),
                        k_mask[:, :].unsqueeze(2).broadcast_to([P, HH, KEYS]), ALU.mult)
                last.then_inc(k_ready, 1)

            def values(i, groups):
                b = i // BLK_PER_B
                for gg in groups:
                    num, _ = group_part(gg)
                    for a in (HI, LO):
                        last = nc.gpsimd.tensor_tensor(
                            v_cur[:, gg, :, a, num].rearrange("p j (h d) -> p j h d", d=DH),
                            v_rows[:, 2 * gg:2 * gg + PAIRS, a, bass.ds(b, 1), :].broadcast_to([P, PAIRS, GH, DH]),
                            v_mask[:, gg, :, :].unsqueeze(3).broadcast_to([P, PAIRS, GH, DH]), ALU.mult)
                if 1 in groups:
                    last.then_inc(v_ready, 1)

            def hidden_low(i, k):
                eng.wait_ge(hf_done, 8 * i + k + 1)
                nc.gpsimd.tensor_tensor(hT[:, LO, k, :], h_f[:, k % 2, :], f(hT[:, HI, k, :]),
                                        ALU.subtract).then_inc(h_lo, 1)

            def x2_plus_bias(i):
                eng.wait_ge(x2_done, 2 * (i + 1))
                plus_row(x2b, x2, b2_bc).then_inc(x2b_done, 1)

            def step(i, ffn, more, stored):
                if ffn:
                    if stored:
                        eng.wait_ge(out_stored, 32 * (i - 1))
                    x2_plus_bias(i - 1)
                    for k in range(FC):
                        hidden_low(i - 1, k)
                if more:
                    eng.wait_ge(rstd_done[0], i + 2)
                    eng.wait_ge(score_ps, 8 * (i + 1))
                    keys(i + 1)
                    normed(0, xn, x_sb, xn_done)
                    eng.wait_ge(pv_ps, 4 * (i + 1))
                    values(i + 1, [0])
                eng.wait_ge(rstd_done[1], i + 1)
                if more:
                    values(i + 1, [1])
                normed(1, xn2, x2, xn2_done)
                if more:
                    plus_row(xb, x_sb, bo_bc).then_inc(xb_done, 1)

            nc.gpsimd.memset(ident[:, :], 0.0).then_inc(setup_pool, 1)
            eng.wait_ge(setup_pool, 1)
            nc.gpsimd.affine_select(out=ident[:, :], in_=ident[:, :], compare_op=ALU.not_equal, fill=1.0,
                                    base=0, pattern=[[-1, P]], channel_multiplier=1).then_inc(setup_pool, 1)
            nc.gpsimd.memset(sel[:, SROW:PW], 0.0)
            eng.wait_ge(setup_pool, 2)
            nc.gpsimd.tensor_copy(sel[:, 0:SROW].rearrange("k (h j) -> k h j", j=KEYS),
                                  ident[0:KEYS, 0:KEYS].unsqueeze(1).broadcast_to([KEYS, HH, KEYS])).then_inc(setup_pool, 1)
            nc.gpsimd.memset(k_mask[:, :], 1.0)
            nc.gpsimd.memset(v_mask[:, :, :, :], 1.0).then_inc(setup_pool, 1)
            eng.wait_ge(setup_pool, 4)
            nc.gpsimd.affine_select(out=k_mask[:, :], in_=k_mask[:, :], compare_op=ALU.is_ge, fill=0.0,
                                    base=0, pattern=[[-DH, HH]], channel_multiplier=1).then_inc(setup_pool, 1)
            row = [[2 * P - GROW, 2], [P, PAIRS], [-KEYS, GH]]
            nc.gpsimd.affine_select(out=v_mask[:, :, :, :], in_=v_mask[:, :, :, :], compare_op=ALU.is_ge, fill=0.0,
                                    base=0, pattern=row, channel_multiplier=1).then_inc(setup_pool, 1)
            eng.wait_ge(setup_pool, 6)
            nc.gpsimd.affine_select(out=k_mask[:, :], in_=k_mask[:, :], compare_op=ALU.is_ge, fill=0.0,
                                    base=DH - 1, pattern=[[DH, HH]], channel_multiplier=-1).then_inc(setup_pool, 1)
            nc.gpsimd.affine_select(out=v_mask[:, :, :, :], in_=v_mask[:, :, :, :], compare_op=ALU.is_ge, fill=0.0,
                                    base=KEYS - 1, pattern=[[-s, n] for s, n in row],
                                    channel_multiplier=-1).then_inc(setup_pool, 1)
            eng.wait_ge(setup_pool, 8)
            for gg in range(2):
                _, den = group_part(gg)
                for a in (HI, LO):
                    dst = v_cur[:, gg, :, a, den].rearrange("p j (h d) -> p j h d", d=DH)
                    mask = v_mask[:, gg, :, :].unsqueeze(3).broadcast_to([P, PAIRS, GH, DH])
                    nc.gpsimd.tensor_scalar(dst, mask, 1.0 if a == HI else 0.0, 0.0, ALU.mult, ALU.add)
            eng.wait_ge(rstd_done[0], 1)
            normed(0, xn, x_sb, xn_done)
            eng.wait_ge(setup_dve, 6)
            keys(0)
            eng.wait_ge(bias_loaded, 16 * (HH + 5))
            plus_row(xb, x_sb, bo_bc).then_inc(xb_done, 1)
            eng.wait_ge(setup_dve, 7)
            values(0, [0, 1])

            step(0, False, True, False)
            step(1, True, True, False)
            with eng.Fori(2, NBLK - 1) as i:
                step(i, True, True, True)
            step(NBLK - 1, True, False, True)
            eng.wait_ge(out_stored, 32 * (NBLK - 1))
            x2_plus_bias(NBLK - 1)
            for k in range(FC):
                hidden_low(NBLK - 1, k)


_INS = ["x", "ctx_1024", "L0_xattn_Wq", "L0_xattn_bq", "L0_xattn_Wk", "L0_xattn_bk", "L0_xattn_Wv",
        "L0_xattn_bv", "L0_xattn_Wo", "L0_xattn_bo", "L0_ffn_W1", "L0_ffn_b1", "L0_ffn_W2", "L0_ffn_b2"]


def kernel(**inputs):
    import numpy as _np
    import concourse.bacc as _bacc
    from concourse import mybir as _mybir
    from concourse.bass_utils import run_bass_kernel_spmd as _run

    nc = _bacc.Bacc("TRN2", target_bir_lowering=False, num_devices=1)
    arrays, args = {}, []
    for name in _INS:
        a = _np.ascontiguousarray(inputs[name])
        arrays[f"in_{name}_dram"] = a
        args.append(nc.dram_tensor(f"in_{name}_dram", a.shape, _mybir.dt.from_np(a.dtype), kind="ExternalInput").ap())
    out = nc.dram_tensor("out_dram", (NB, SEQ, D), F32, kind="ExternalOutput").ap()
    xattn_ffn(nc, *args, out)
    r = _run(nc, [arrays], core_ids=[0])
    return r.results[0]["out_dram"]
```

```python
import concourse.bass as bass
from concourse import mybir
from contextlib import ExitStack

F32 = mybir.dt.float32
F32R = mybir.dt.float32r
ALU = mybir.AluOpType
ACT = mybir.ActivationFunctionType
AX = mybir.AxisListType

P = 128
NB, SEQ, D = 4, 1024, 256
KEYS = 77
HEADS, DH = 16, 16
FF = 1024
BLK = 512
NT = BLK // P
NBLK = NB * SEQ // BLK
BLK_PER_B = SEQ // BLK
KC = D // P
FC = FF // P
HH = P // DH
HALVES = HEADS // HH
GH = HH // 2
SROW = HH * KEYS
GROUPS = HEADS // GH
GD = GH * DH
GROW = GH * KEYS
PC = -(-SROW // P)
PW = PC * P
PAIRS = 3
UNITS = HALVES * NT
SCALE = float(DH) ** -0.5
EPS = 1e-5
HI, LO = 0, 1
PASSES = ((HI, HI), (LO, HI), (HI, LO))


def xattn_ffn(nc, x, ctx, Wq, bq, Wk, bk, Wv, bv, Wo, bo, W1, b1, W2, b2, out):
    x_blk = x.rearrange("b (c t p) d -> (b c) p t d", t=NT, p=P)
    out_blk = out.rearrange("b (c t p) d -> (b c) p t d", t=NT, p=P)
    stack = ExitStack()

    def sb(name, shape, dt=F32):
        return stack.enter_context(nc.sbuf_tensor(name, shape, dt))

    def sem(name):
        return stack.enter_context(nc.semaphore(name))

    def f(ap):
        return ap.bitcast(F32)

    with stack:
        ident = sb("ident", [P, P])
        wq = sb("wq", [P, 2, KC, D], F32R)
        wo = sb("wo", [P, 2, KC, D], F32R)
        w1 = sb("w1", [P, 2, KC, FF], F32R)
        w2 = sb("w2", [P, 2, FC, D], F32R)
        bq_sb = sb("bq_sb", [GD, GROUPS])
        b1_sb = sb("b1_sb", [P, FC])
        bk_sb = sb("bk_sb", [P, 1])
        bo_bc = sb("bo_bc", [P, D])
        b2_bc = sb("b2_bc", [P, D])
        bv_bc = sb("bv_bc", [KEYS, DH])
        eps_sb = sb("eps_sb", [P, 1])
        k_rep = sb("k_rep", [P, 2, NB * KEYS])
        v_rows = sb("v_rows", [P, PC, 2, NB, DH])
        p_mask = sb("p_mask", [P, HH])
        k_mask = sb("k_mask", [P, GH])
        v_mask = sb("v_mask", [P, 2, PAIRS, GH])
        k_cur = sb("k_cur", [P, 2, GH, KEYS], F32R)
        v_cur = sb("v_cur", [P, 2, PAIRS, 2, P], F32R)
        x_sb = sb("x_sb", [P, NT, D])
        xb = sb("xb", [P, NT, D])
        xn = sb("xn", [P, NT, D])
        xnT = sb("xnT", [P, 2, KC, BLK], F32R)
        qT = sb("qT", [P, GROUPS, BLK], F32R)
        s_sub = sb("s_sub", [P, 2, PW])
        e_f = sb("e_f", [P, 2, PW])
        pT = sb("pT", [P, 2, HALVES, PC, BLK], F32R)
        att = sb("att", [P, HALVES, BLK])
        attT = sb("attT", [P, 2, HALVES, BLK], F32R)
        smax = sb("smax", [P, 2, HH])
        x2 = sb("x2", [P, NT, D])
        x2b = sb("x2b", [P, NT, D])
        xn2 = sb("xn2", [P, NT, D])
        x2nT = sb("x2nT", [P, 2, KC, BLK], F32R)
        h_f = sb("h_f", [P, 2, BLK])
        st = [sb(f"st{n}", [P, NT, 6]) for n in (1, 2)]
        mv = [sb(f"mv{n}", [P, NT, 2]) for n in (1, 2)]
        nmean = [sb(f"nmean{n}", [P, NT]) for n in (1, 2)]
        lnv = [sb(f"lnv{n}", [P, NT]) for n in (1, 2)]
        rstd = [sb(f"rstd{n}", [P, NT]) for n in (1, 2)]
        y2 = [sb(f"y2_{n}", [P, NT]) for n in (1, 2)]
        vy2 = [sb(f"vy2_{n}", [P, NT]) for n in (1, 2)]
        corr = [sb(f"corr{n}", [P, NT]) for n in (1, 2)]
        istd = [sb(f"istd{n}", [P, NT]) for n in (1, 2)]
        with ExitStack() as early:
            def tmp(name, shape):
                return early.enter_context(nc.sbuf_tensor(name, shape, F32))
            w1_raw = tmp("w1_raw", [P, KC, FF])
            w2_raw = tmp("w2_raw", [P, FC, D])
            wo_raw = tmp("wo_raw", [P, KC, D])
            wq_raw = tmp("wq_raw", [P, KC, D])
            ctx_sb = tmp("ctx_sb", [KEYS, NB, D])
            ctxT = tmp("ctxT", [P, KC, NB * KEYS])
            wk_raw = tmp("wk_raw", [P, KC, DH])
            wk_rep = tmp("wk_rep", [P, KC, HH, DH])
            wv_sb = tmp("wv_sb", [P, KC, DH])
            v_f = tmp("v_f", [KEYS, NB, DH])
            v_all = tmp("v_all", [KEYS, 2, NB, DH])
        hT = sb("hT", [P, 2, FC, BLK], F32R)
        sel = x2b[0:KEYS, :, :].rearrange("k t d -> k (t d)")[:, 0:PW]

        s_ps = stack.enter_context(nc.psum_tensor("s_ps", [P, 4, 512], F32))
        t_ps = stack.enter_context(nc.psum_tensor("t_ps", [P, 2, 512], F32))
        g_ps = stack.enter_context(nc.psum_tensor("g_ps", [P, 2, 512], F32))
        t_flat = t_ps[:, :, :].rearrange("p a b -> p (a b)")

        kv_loaded, wk_loaded = sem("kv_loaded"), sem("wk_loaded")
        kv_bias_loaded, bias_loaded, ffn_bias_loaded = sem("kv_bias_loaded"), sem("bias_loaded"), sem("ffn_bias_loaded")
        wq_loaded, wo_loaded = sem("wq_loaded"), sem("wo_loaded")
        w1_loaded, w2_loaded = sem("w1_loaded"), sem("w2_loaded")
        x_loaded, out_stored = sem("x_loaded"), sem("out_stored")
        setup_pool, setup_dve, setup_act, setup_pe = (sem(f"setup_{e}") for e in ("pool", "dve", "act", "pe"))
        w_hi, w_lo = sem("w_hi"), sem("w_lo")
        stats_done = [sem(f"stats{n}_done") for n in (1, 2)]
        aggr_done = [sem(f"aggr{n}_done") for n in (1, 2)]
        nmean_done = [sem(f"nmean{n}_done") for n in (1, 2)]
        lnv_done = [sem(f"lnv{n}_done") for n in (1, 2)]
        rstd_done = [sem(f"rstd{n}_done") for n in (1, 2)]
        refined = [sem(f"refined{n}") for n in (1, 2)]
        xn_done, xn2_done = sem("xn_done"), sem("xn2_done")
        xb_done, x2b_done = sem("xb_done"), sem("x2b_done")
        xnT_ps, xnT_hi, xnT_lo = sem("xnT_ps"), sem("xnT_hi"), sem("xnT_lo")
        q_ps, q_hi, q_lo = sem("q_ps"), sem("q_hi"), sem("q_lo")
        k_ready, v_ready = sem("k_ready"), sem("v_ready")
        score_ps, max_done, sub_done = sem("score_ps"), sem("max_done"), sem("sub_done")
        subT_ps, p_hi, e_done, p_lo = sem("subT_ps"), sem("p_hi"), sem("e_done"), sem("p_lo")
        pv_ps, log_done, inv_done, att_done = sem("pv_ps"), sem("log_done"), sem("inv_done"), sem("att_done")
        att_hi, att_lo = sem("att_hi"), sem("att_lo")
        o_ps, x2_done = sem("o_ps"), sem("x2_done")
        x2nT_ps, x2nT_hi, x2nT_lo = sem("x2nT_ps"), sem("x2nT_hi"), sem("x2nT_lo")
        h_ps, h_hi, hf_done, h_lo = sem("h_ps"), sem("h_hi"), sem("hf_done"), sem("h_lo")
        y_ps, out_done = sem("y_ps"), sem("out_done")

        block = stack.enter_context(nc.Block())

        w1_pieces = [(w1_raw[:, c, h * 512:(h + 1) * 512], w1[:, HI, c, h * 512:(h + 1) * 512],
                      w1[:, LO, c, h * 512:(h + 1) * 512], w1_loaded) for c in range(KC) for h in range(2)]
        w2_pieces = [(w2_raw[:, c:c + 2, :], w2[:, HI, c:c + 2, :], w2[:, LO, c:c + 2, :], w2_loaded)
                     for c in range(0, FC, 2)]
        pieces = w1_pieces + w2_pieces
        assert len(pieces) == UNITS

        def group_part(g):
            a = (g % 2) * 64
            return slice(a, a + 64), slice(64 - a, 128 - a)

        @block.sync
        def _(eng):
            eng.dma_start(x_sb[:, :, :], x_blk[0]).then_inc(x_loaded, 16)
            eng.dma_start(wq_raw[:, :, :], Wq.rearrange("(c p) n -> p c n", p=P)).then_inc(wq_loaded, 16)
            for h in range(HH):
                eng.dma_start(bk_sb[h * DH:(h + 1) * DH, :], bk.rearrange("(d a) -> d a", a=1)).then_inc(kv_bias_loaded, 16)
            eng.dma_start(bv_bc[:, :], bv.partition_broadcast(KEYS)).then_inc(kv_bias_loaded, 16)
            eng.dma_start(bq_sb[:, :], bq.rearrange("(g p) -> p g", p=GD), allow_slow_non_contiguous=True).then_inc(bias_loaded, 16)
            eng.dma_start(bo_bc[:, :], bo.partition_broadcast(P)).then_inc(bias_loaded, 16)
            eng.dma_start(wo_raw[:, :, :], Wo.rearrange("(c p) n -> p c n", p=P)).then_inc(wo_loaded, 16)
            eng.dma_start(w1_raw[:, :, :], W1.rearrange("(c p) n -> p c n", p=P)).then_inc(w1_loaded, 16)
            eng.dma_start(w2_raw[:, :, :], W2.rearrange("(c p) n -> p c n", p=P)).then_inc(w2_loaded, 16)
            eng.dma_start(b1_sb[:, :], b1.rearrange("(m p) -> p m", p=P), allow_slow_non_contiguous=True).then_inc(ffn_bias_loaded, 16)
            eng.dma_start(b2_bc[:, :], b2.partition_broadcast(P)).then_inc(ffn_bias_loaded, 16)

            def load_next(i):
                eng.wait_ge(xb_done, i + 1)
                eng.dma_start(x_sb[:, :, :], x_blk[i + 1]).then_inc(x_loaded, 16)

            def store(i):
                for tp in range(2):
                    eng.wait_ge(out_done, 2 * i + tp + 1)
                    eng.dma_start(out_blk[i][:, 2 * tp:2 * tp + 2, :],
                                  x2b[:, 2 * tp:2 * tp + 2, :]).then_inc(out_stored, 16)

            load_next(0)
            load_next(1)
            store(0)
            with eng.Fori(2, NBLK - 1) as i:
                load_next(i)
                store(i - 1)
            store(NBLK - 2)
            store(NBLK - 1)
            eng.wait_ge(out_stored, 32 * NBLK)

        @block.tensor
        def _(eng):
            def mm3(o, lhs, rhs, steps):
                n = len(steps) * len(PASSES)
                j = 0
                for s in steps:
                    for a, b in PASSES:
                        last = nc.tensor.matmul(o, lhs(a, s), rhs(b, s), start=(j == 0), stop=(j == n - 1))
                        j += 1
                return last

            def transpose_rows(src, done):
                for c in range(KC):
                    for t in range(NT):
                        last = nc.tensor.transpose(t_ps[:, c, t * P:(t + 1) * P],
                                                   src[:, t, c * P:(c + 1) * P], ident[:, :])
                    last.then_inc(done, 1)

            def queries():
                for m in range(KC):
                    mm3(s_ps[:, m, :], lambda a, c: wq[:, a, c, m * P:(m + 1) * P],
                        lambda b, c: xnT[:, b, c, :], range(KC)).then_inc(q_ps, 1)

            def scores(u):
                hf, t = divmod(u, NT)
                for j in range(2):
                    for a in (HI, LO):
                        last = nc.tensor.matmul(s_ps[:, 2 * (u % 2) + j, 0:GROW],
                                                qT[:, 2 * hf + j, t * P:(t + 1) * P],
                                                k_cur[:, a, :, :].rearrange("p h k -> p (h k)"),
                                                start=(a == HI), stop=(a == LO))
                last.then_inc(score_ps, 1)

            def ffn_in(k):
                mm3(g_ps[:, k % 2, :], lambda a, c: w1[:, a, c, k * P:(k + 1) * P],
                    lambda b, c: x2nT[:, b, c, :], range(KC)).then_inc(h_ps, 1)

            def ffn_out(tp, ps=g_ps, waits=None):
                def hidden_rows(a, k, t):
                    if waits is not None and t == 2 * tp and a == HI:
                        eng.wait_ge(h_lo, waits + k + 1)
                    return hT[:, a, k, t * P:(t + 1) * P]

                for t in (2 * tp, 2 * tp + 1):
                    last = mm3(ps[:, tp, (t % 2) * D:(t % 2 + 1) * D],
                               lambda a, k: hidden_rows(a, k, t),
                               lambda b, k: w2[:, b, k, :], range(FC))
                last.then_inc(y_ps, 1)

            def step(i, ffn, more):
                if ffn:
                    eng.wait_ge(x2nT_lo, 2 * i)
                for k in range(UNITS):
                    if ffn:
                        if k >= 2:
                            eng.wait_ge(hf_done, 8 * (i - 1) + k - 1)
                        ffn_in(k)
                    eng.wait_ge(sub_done, 8 * i + k + 1)
                    if k >= 1:
                        eng.wait_ge(e_done, 8 * i + k)
                    for c in range(PC):
                        last = nc.tensor.transpose(t_flat[:, c * P:(c + 1) * P],
                                                   s_sub[:, k % 2, c * P:(c + 1) * P], ident[:, :])
                    last.then_inc(subT_ps, 1)
                    if k + 2 < UNITS:
                        scores(k + 2)
                eng.wait_ge(v_ready, i + 1)
                for g in range(4):
                    hf, gg = divmod(g, 2)
                    if gg == 0:
                        eng.wait_ge(p_lo, 8 * i + NT * (hf + 1))
                    mm3(s_ps[:, g, :], lambda a, j: v_cur[:, gg, j, a, :],
                        lambda b, j: pT[:, b, hf, 2 * gg + j, :], range(PAIRS)).then_inc(pv_ps, 1)
                if more:
                    eng.wait_ge(xn_done, 4 * (i + 2))
                    transpose_rows(xn, xnT_ps)
                if ffn:
                    eng.wait_ge(h_lo, 8 * i)
                    ffn_out(0)
                if not ffn:
                    eng.wait_ge(w_lo, 2)
                if more:
                    eng.wait_ge(xnT_lo, 2 * (i + 2))
                eng.wait_ge(att_lo, 2 * (i + 1))
                for tp in range(2):
                    for t in (2 * tp, 2 * tp + 1):
                        last = mm3(t_ps[:, tp, (t % 2) * D:(t % 2 + 1) * D],
                                   lambda a, c: attT[:, a, c, t * P:(t + 1) * P],
                                   lambda b, c: wo[:, b, c, :], range(KC))
                    last.then_inc(o_ps, 1)
                if more:
                    queries()
                if ffn:
                    ffn_out(1)
                eng.wait_ge(xn2_done, 4 * (i + 1))
                transpose_rows(xn2, x2nT_ps)
                if more:
                    eng.wait_ge(q_lo, GROUPS * (i + 2))
                    eng.wait_ge(k_ready, i + 2)
                    scores(0)
                    scores(1)

            eng.wait_ge(setup_pool, 2)
            eng.wait_ge(kv_loaded, 16)
            for c in range(KC):
                for b in range(NB):
                    last = nc.tensor.transpose(s_ps[:, c, b * KEYS:(b + 1) * KEYS],
                                               ctx_sb[:, b, c * P:(c + 1) * P], ident[0:KEYS, 0:KEYS])
            last.then_inc(setup_pe, 1)
            eng.wait_ge(setup_act, 1)
            eng.wait_ge(setup_dve, 2)
            for c in range(KC):
                last = nc.tensor.matmul(s_ps[:, 2, 0:NB * KEYS], wk_rep[:, c, :, :].rearrange("p h d -> p (h d)"),
                                        ctxT[:, c, :], start=(c == 0), stop=(c == KC - 1))
            last.then_inc(setup_pe, 1)
            for b in range(NB):
                for c in range(KC):
                    last = nc.tensor.matmul(s_ps[0:KEYS, 3, b * DH:(b + 1) * DH],
                                            ctxT[:, c, b * KEYS:(b + 1) * KEYS], wv_sb[:, c, :],
                                            start=(c == 0), stop=(c == KC - 1))
            last.then_inc(setup_pe, 1)
            eng.wait_ge(xn_done, 4)
            transpose_rows(xn, xnT_ps)
            eng.wait_ge(xnT_lo, 2)
            eng.wait_ge(w_lo, 1)
            queries()
            eng.wait_ge(setup_dve, 5)
            eng.wait_ge(setup_pool, 4)
            for c in range(PC):
                last = nc.tensor.matmul(g_ps[:, c // 4, (c % 4) * P:(c % 4 + 1) * P],
                                        sel[:, c * P:(c + 1) * P],
                                        v_all[:, :, :, :].rearrange("k a b d -> k (a b d)"),
                                        start=True, stop=True)
            last.then_inc(setup_pe, 1)
            eng.wait_ge(q_lo, GROUPS)
            eng.wait_ge(k_ready, 1)
            scores(0)
            scores(1)

            step(0, False, True)
            step(1, True, True)
            with eng.Fori(2, NBLK - 1) as i:
                step(i, True, True)
            step(NBLK - 1, True, False)
            eng.wait_ge(x2nT_lo, 2 * NBLK)
            for k in range(FC):
                if k >= 2:
                    eng.wait_ge(hf_done, 8 * (NBLK - 1) + k - 1)
                ffn_in(k)
            ffn_out(0, t_ps, 8 * (NBLK - 1))
            ffn_out(1, t_ps)

        @block.scalar
        def _(eng):
            eng.dma_start(ctx_sb[:, :, :], ctx.rearrange("b k d -> k b d")).then_inc(kv_loaded, 16)
            eng.dma_start(wk_raw[:, :, :], Wk.rearrange("(c p) n -> p c n", p=P)).then_inc(wk_loaded, 16)
            eng.dma_start(wv_sb[:, :, :], Wv.rearrange("(c p) n -> p c n", p=P)).then_inc(wk_loaded, 16)
            eng.preload_act_table_set("natural_log_exp_and_others")

            def inv_std(n, i):
                eng.wait_ge(nmean_done[n], i + 1)
                nc.scalar.activation(lnv[n][:, :], mv[n][:, :, 1], ACT.Ln, bias=eps_sb[:, :]).then_inc(lnv_done[n], 1)
                eng.wait_ge(lnv_done[n], i + 1)
                nc.scalar.activation(rstd[n][:, :], lnv[n][:, :], ACT.Exp, scale=-0.5).then_inc(rstd_done[n], 1)

            def rows_high(dst, ps_done, done, i):
                for c in range(KC):
                    eng.wait_ge(ps_done, 2 * i + c + 1)
                    nc.scalar.activation(dst[:, HI, c, :], t_ps[:, c, :], ACT.Copy).then_inc(done, 1)

            def query_high(i, m):
                eng.wait_ge(q_ps, 2 * i + m + 1)
                for j in range(2):
                    nc.scalar.activation(qT[0:GD, 2 * m + j, :], s_ps[j * GD:(j + 1) * GD, m, :], ACT.Identity,
                                         bias=bq_sb[:, 2 * m + j:2 * m + j + 1]).then_inc(q_hi, 1)

            def hidden(i, k):
                eng.wait_ge(h_ps, 8 * i + k + 1)
                nc.scalar.activation(hT[:, HI, k, :], g_ps[:, k % 2, :], ACT.Relu,
                                     bias=b1_sb[:, k:k + 1]).then_inc(h_hi, 1)
                if k >= 2:
                    eng.wait_ge(h_lo, 8 * i + k - 1)
                nc.scalar.activation(h_f[:, k % 2, :], g_ps[:, k % 2, :], ACT.Relu,
                                     bias=b1_sb[:, k:k + 1]).then_inc(hf_done, 1)

            def step(i, ffn, more):
                for k in range(UNITS):
                    if ffn:
                        hidden(i - 1, k)
                    hf, t = divmod(k, NT)
                    eng.wait_ge(subT_ps, 8 * i + k + 1)
                    src = t_flat[:, 0:PW].rearrange("p (c t) -> p c t", t=P)
                    nc.scalar.activation(pT[:, HI, hf, :, t * P:(t + 1) * P], src, ACT.Exp,
                                         scale=SCALE).then_inc(p_hi, 1)
                    if k >= 2:
                        eng.wait_ge(p_lo, 8 * i + k - 1)
                    nc.scalar.activation(e_f[:, k % 2, :], t_flat[:, 0:PW], ACT.Exp,
                                         scale=SCALE).then_inc(e_done, 1)
                    if not ffn:
                        raw, high, _, loaded = pieces[k]
                        eng.wait_ge(loaded, 16)
                        nc.scalar.activation(high, raw, ACT.Copy).then_inc(w_hi, 1)
                if more:
                    inv_std(0, i + 1)
                for g in range(4):
                    num, den = group_part(g)
                    hf = g // 2
                    eng.wait_ge(pv_ps, 4 * i + g + 1)
                    nc.scalar.activation(att[num, hf, :], s_ps[den, g, :], ACT.Ln).then_inc(log_done, 1)
                    eng.wait_ge(log_done, 4 * i + g + 1)
                    nc.scalar.activation(att[num, hf, :], att[num, hf, :], ACT.Exp, scale=-1.0).then_inc(inv_done, 1)
                    if g == 2:
                        att_high(i, 0)
                if more:
                    rows_high(xnT, xnT_ps, xnT_hi, i + 1)
                att_high(i, 1)
                if more:
                    query_high(i + 1, 0)
                    inv_std(1, i)
                    query_high(i + 1, 1)
                else:
                    inv_std(1, i)
                rows_high(x2nT, x2nT_ps, x2nT_hi, i)

            def att_high(i, hf):
                eng.wait_ge(att_done, 4 * i + 2 * hf + 2)
                nc.scalar.activation(attT[:, HI, hf, :], att[:, hf, :], ACT.Copy).then_inc(att_hi, 1)

            eng.wait_ge(setup_pe, 1)
            nc.scalar.activation(ctxT[:, :, :], s_ps[:, 0:KC, 0:NB * KEYS], ACT.Copy).then_inc(setup_act, 1)
            eng.wait_ge(setup_dve, 2)
            inv_std(0, 0)
            eng.wait_ge(kv_bias_loaded, 16 * (HH + 1))
            eng.wait_ge(setup_pe, 2)
            nc.scalar.activation(k_rep[:, HI, :].bitcast(F32R), s_ps[:, 2, 0:NB * KEYS], ACT.Identity,
                                 bias=bk_sb[:, :]).then_inc(setup_act, 1)
            eng.wait_ge(wq_loaded, 16)
            nc.scalar.activation(wq[:, HI, :, :], wq_raw[:, :, :], ACT.Copy).then_inc(w_hi, 1)
            rows_high(xnT, xnT_ps, xnT_hi, 0)
            eng.wait_ge(wo_loaded, 16)
            nc.scalar.activation(wo[:, HI, :, :], wo_raw[:, :, :], ACT.Copy).then_inc(w_hi, 1)
            eng.wait_ge(bias_loaded, 32)
            query_high(0, 0)
            query_high(0, 1)

            step(0, False, True)
            eng.wait_ge(ffn_bias_loaded, 32)
            step(1, True, True)
            with eng.Fori(2, NBLK - 1) as i:
                step(i, True, True)
            step(NBLK - 1, True, False)
            for k in range(FC):
                hidden(NBLK - 1, k)

        @block.vector
        def _(eng):
            def stats(n, src, i, tiles):
                for t in tiles:
                    nc.vector.bn_stats(st[n][:, t, :], src[:, t, :]).then_inc(stats_done[n], 1)

            def moments(n, i):
                for t in range(NT):
                    nc.vector.bn_aggr(mv[n][:, t, :], st[n][:, t, :]).then_inc(aggr_done[n], 1)
                eng.wait_ge(aggr_done[n], 4 * (i + 1))
                nc.vector.tensor_scalar(nmean[n][:, :], mv[n][:, :, 0], -1.0, None, ALU.mult).then_inc(nmean_done[n], 1)

            def normed(n, dst, src, done, i):
                eng.wait_ge(rstd_done[n], i + 1)
                nc.vector.tensor_tensor(y2[n][:, :], rstd[n][:, :], rstd[n][:, :], ALU.mult).then_inc(refined[n], 1)
                eng.wait_ge(refined[n], 4 * i + 1)
                nc.vector.scalar_tensor_tensor(vy2[n][:, :], mv[n][:, :, 1], EPS, y2[n][:, :],
                                               ALU.add, ALU.mult).then_inc(refined[n], 1)
                eng.wait_ge(refined[n], 4 * i + 2)
                nc.vector.tensor_scalar(corr[n][:, :], vy2[n][:, :], -0.5, 1.5, ALU.mult, ALU.add).then_inc(refined[n], 1)
                eng.wait_ge(refined[n], 4 * i + 3)
                nc.vector.tensor_tensor(istd[n][:, :], rstd[n][:, :], corr[n][:, :], ALU.mult).then_inc(refined[n], 1)
                eng.wait_ge(refined[n], 4 * i + 4)
                for t in range(NT):
                    nc.vector.tensor_scalar(dst[:, t, :], src[:, t, :], nmean[n][:, t:t + 1],
                                            istd[n][:, t:t + 1], ALU.add, ALU.mult).then_inc(done, 1)

            def rows_low(dst, high_done, done, i):
                for c in range(KC):
                    eng.wait_ge(high_done, 2 * i + c + 1)
                    nc.vector.tensor_tensor(dst[:, LO, c, :], t_ps[:, c, :], f(dst[:, HI, c, :]),
                                            ALU.subtract).then_inc(done, 1)

            def query_low(i, m):
                for j in range(2):
                    g = 2 * m + j
                    eng.wait_ge(q_hi, GROUPS * i + g + 1)
                    nc.vector.scalar_tensor_tensor(qT[GD:P, g, :], s_ps[j * GD:(j + 1) * GD, m, :],
                                                   bq_sb[:, g:g + 1], f(qT[0:GD, g, :]),
                                                   ALU.add, ALU.subtract).then_inc(q_lo, 1)

            def prob_low(i, k):
                hf, t = divmod(k, NT)
                eng.wait_ge(e_done, 8 * i + k + 1)
                nc.vector.tensor_tensor(pT[:, LO, hf, :, t * P:(t + 1) * P],
                                        e_f[:, k % 2, :].rearrange("p (c t) -> p c t", t=P),
                                        f(pT[:, HI, hf, :, t * P:(t + 1) * P]), ALU.subtract).then_inc(p_lo, 1)

            def att_low(i, hf):
                eng.wait_ge(att_hi, 2 * i + hf + 1)
                nc.vector.tensor_tensor(attT[:, LO, hf, :], att[:, hf, :], f(attT[:, HI, hf, :]),
                                        ALU.subtract).then_inc(att_lo, 1)

            def result(i, tp, ps=g_ps):
                eng.wait_ge(y_ps, 2 * i + tp + 1)
                nc.vector.tensor_tensor(x2b[:, 2 * tp:2 * tp + 2, :],
                                        ps[:, tp, :].rearrange("p (t d) -> p t d", d=D),
                                        x2b[:, 2 * tp:2 * tp + 2, :], ALU.add).then_inc(out_done, 1)

            def weight_low(k):
                raw, high, low, _ = pieces[k]
                eng.wait_ge(w_hi, 2 + k + 1)
                nc.vector.tensor_tensor(low, raw, f(high), ALU.subtract).then_inc(w_lo, 1)

            def step(i, ffn, more):
                for k in range(UNITS):
                    eng.wait_ge(score_ps, 8 * i + k + 1)
                    s = s_ps[:, 2 * (k % 2):2 * (k % 2) + 2, 0:GROW].rearrange("p j (h k) -> p j h k", k=KEYS)
                    m = smax[:, k % 2, :].rearrange("p (j h) -> p j h", j=2)
                    nc.vector.tensor_reduce(m, s, AX.X, ALU.max).then_inc(max_done, 1)
                    if more and k == 6:
                        eng.wait_ge(stats_done[0], 4 * (i + 2))
                    if k >= 2:
                        prob_low(i, k - 2)
                        eng.wait_ge(subT_ps, 8 * i + k - 1)
                    eng.wait_ge(max_done, 8 * i + k + 1)
                    nc.vector.tensor_tensor(s_sub[:, k % 2, 0:SROW].rearrange("p (j h k) -> p j h k", j=2, k=KEYS),
                                            s, m.unsqueeze(3).broadcast_to([P, 2, GH, KEYS]),
                                            ALU.subtract).then_inc(sub_done, 1)
                    if more and 2 <= k < 2 + NT:
                        if k == 2:
                            eng.wait_ge(x_loaded, 16 * (i + 2))
                        stats(0, x_sb, i + 1, [k - 2])
                    if more and k == 6:
                        moments(0, i + 1)
                    if not ffn and k >= 1:
                        weight_low(k - 1)
                prob_low(i, UNITS - 2)
                prob_low(i, UNITS - 1)
                if not ffn:
                    weight_low(UNITS - 1)
                if more:
                    normed(0, xn, x_sb, xn_done, i + 1)
                for g in range(4):
                    num, _ = group_part(g)
                    eng.wait_ge(inv_done, 4 * i + g + 1)
                    nc.vector.tensor_tensor(att[num, g // 2, :], s_ps[num, g, :], att[num, g // 2, :],
                                            ALU.mult).then_inc(att_done, 1)
                    if g == 2:
                        att_low(i, 0)
                if more:
                    rows_low(xnT, xnT_hi, xnT_lo, i + 1)
                att_low(i, 1)
                if ffn:
                    result(i - 1, 0)
                    eng.wait_ge(x2b_done, i)
                for tp in range(2):
                    eng.wait_ge(o_ps, 2 * i + tp + 1)
                    nc.vector.tensor_tensor(x2[:, 2 * tp:2 * tp + 2, :],
                                            t_ps[:, tp, :].rearrange("p (t d) -> p t d", d=D),
                                            xb[:, 2 * tp:2 * tp + 2, :], ALU.add).then_inc(x2_done, 1)
                for tp in range(2):
                    eng.wait_ge(x2_done, 2 * i + tp + 1)
                    stats(1, x2, i, (2 * tp, 2 * tp + 1))
                eng.wait_ge(stats_done[1], 4 * (i + 1))
                if more:
                    query_low(i + 1, 0)
                moments(1, i)
                if more:
                    query_low(i + 1, 1)
                normed(1, xn2, x2, xn2_done, i)
                if ffn:
                    result(i - 1, 1)
                rows_low(x2nT, x2nT_hi, x2nT_lo, i)

            nc.vector.memset(eps_sb[:, :], EPS)
            nc.vector.memset(s_sub[:, :, SROW:PW], 0.0).then_inc(setup_dve, 1)
            eng.wait_ge(wk_loaded, 32)
            nc.vector.tensor_copy(wk_rep[:, :, :, :],
                                  wk_raw[:, :, :].unsqueeze(2).broadcast_to([P, KC, HH, DH])).then_inc(setup_dve, 1)
            eng.wait_ge(x_loaded, 16)
            stats(0, x_sb, 0, range(NT))
            eng.wait_ge(stats_done[0], 4)
            moments(0, 0)
            normed(0, xn, x_sb, xn_done, 0)
            eng.wait_ge(kv_bias_loaded, 16 * (HH + 1))
            eng.wait_ge(setup_pe, 3)
            nc.vector.tensor_tensor(v_f[:, :, :], s_ps[0:KEYS, 3, 0:NB * DH].rearrange("k (b d) -> k b d", d=DH),
                                    bv_bc[:, :].unsqueeze(1).broadcast_to([KEYS, NB, DH]), ALU.add).then_inc(setup_dve, 1)
            eng.wait_ge(setup_dve, 3)
            nc.vector.tensor_copy(v_all[:, HI, :, :].bitcast(F32R), v_f[:, :, :]).then_inc(setup_dve, 1)
            eng.wait_ge(setup_dve, 4)
            nc.vector.tensor_tensor(v_all[:, LO, :, :].bitcast(F32R), v_f[:, :, :], v_all[:, HI, :, :],
                                    ALU.subtract).then_inc(setup_dve, 1)
            eng.wait_ge(setup_act, 2)
            nc.vector.scalar_tensor_tensor(k_rep[:, LO, :].bitcast(F32R), s_ps[:, 2, 0:NB * KEYS], bk_sb[:, :],
                                           k_rep[:, HI, :], ALU.add, ALU.subtract).then_inc(setup_dve, 1)
            eng.wait_ge(w_hi, 1)
            nc.vector.tensor_tensor(wq[:, LO, :, :], wq_raw[:, :, :], f(wq[:, HI, :, :]),
                                    ALU.subtract).then_inc(w_lo, 1)
            rows_low(xnT, xnT_hi, xnT_lo, 0)
            eng.wait_ge(w_hi, 2)
            nc.vector.tensor_tensor(wo[:, LO, :, :], wo_raw[:, :, :], f(wo[:, HI, :, :]),
                                    ALU.subtract).then_inc(w_lo, 1)
            eng.wait_ge(bias_loaded, 32)
            query_low(0, 0)
            query_low(0, 1)
            eng.wait_ge(setup_pe, 4)
            nc.vector.tensor_copy(v_rows[:, 0:4, :, :, :].rearrange("p c a b d -> p (c a b d)"),
                                  g_ps[:, 0, :])
            nc.vector.tensor_copy(v_rows[:, 4, :, :, :].rearrange("p a b d -> p (a b d)"),
                                  g_ps[:, 1, 0:P]).then_inc(setup_dve, 1)

            step(0, False, True)
            step(1, True, True)
            with eng.Fori(2, NBLK - 1) as i:
                step(i, True, True)
            step(NBLK - 1, True, False)
            result(NBLK - 1, 0, t_ps)
            result(NBLK - 1, 1, t_ps)

        @block.gpsimd
        def _(eng):
            def plus_row(dst, src, row):
                return nc.gpsimd.tensor_tensor(dst[:, :, :], src[:, :, :],
                                               row[:, :].unsqueeze(1).broadcast_to([P, NT, D]), ALU.add)

            def keys(i):
                b = i // BLK_PER_B
                for a in (HI, LO):
                    last = nc.gpsimd.tensor_tensor(
                        k_cur[:, a, :, :], k_rep[:, a, bass.ds(b * KEYS, KEYS)].unsqueeze(1).broadcast_to([P, GH, KEYS]),
                        k_mask[:, :].unsqueeze(2).broadcast_to([P, GH, KEYS]), ALU.mult)
                last.then_inc(k_ready, 1)

            def values(i):
                b = i // BLK_PER_B
                for gg in range(2):
                    num, _ = group_part(gg)
                    for a in (HI, LO):
                        last = nc.gpsimd.tensor_tensor(
                            v_cur[:, gg, :, a, num].rearrange("p j (h d) -> p j h d", d=DH),
                            v_rows[:, 2 * gg:2 * gg + PAIRS, a, bass.ds(b, 1), :].broadcast_to([P, PAIRS, GH, DH]),
                            v_mask[:, gg, :, :].unsqueeze(3).broadcast_to([P, PAIRS, GH, DH]), ALU.mult)
                last.then_inc(v_ready, 1)

            def hidden_low(i, k):
                eng.wait_ge(hf_done, 8 * i + k + 1)
                nc.gpsimd.tensor_tensor(hT[:, LO, k, :], h_f[:, k % 2, :], f(hT[:, HI, k, :]),
                                        ALU.subtract).then_inc(h_lo, 1)

            def x2_plus_bias(i):
                eng.wait_ge(x2_done, 2 * (i + 1))
                plus_row(x2b, x2, b2_bc).then_inc(x2b_done, 1)

            def step(i, ffn, more, stored):
                if ffn:
                    if stored:
                        eng.wait_ge(out_stored, 32 * (i - 1))
                    x2_plus_bias(i - 1)
                    for k in range(FC):
                        hidden_low(i - 1, k)
                if more:
                    eng.wait_ge(score_ps, 8 * (i + 1))
                    keys(i + 1)
                    eng.wait_ge(pv_ps, 4 * (i + 1))
                    values(i + 1)
                    eng.wait_ge(x2_done, 2 * (i + 1))
                    eng.wait_ge(xn_done, 4 * (i + 2))
                    plus_row(xb, x_sb, bo_bc).then_inc(xb_done, 1)

            nc.gpsimd.memset(ident[:, :], 0.0).then_inc(setup_pool, 1)
            eng.wait_ge(setup_pool, 1)
            nc.gpsimd.affine_select(out=ident[:, :], in_=ident[:, :], compare_op=ALU.not_equal, fill=1.0,
                                    base=0, pattern=[[-1, P]], channel_multiplier=1).then_inc(setup_pool, 1)
            nc.gpsimd.memset(sel[:, SROW:PW], 0.0)
            eng.wait_ge(setup_pool, 2)
            nc.gpsimd.tensor_copy(sel[:, 0:SROW].rearrange("k (h j) -> k h j", j=KEYS),
                                  ident[0:KEYS, 0:KEYS].unsqueeze(1).broadcast_to([KEYS, HH, KEYS])).then_inc(setup_pool, 1)
            nc.gpsimd.memset(p_mask[:, :], 1.0)
            nc.gpsimd.memset(v_mask[:, :, :, :], 1.0).then_inc(setup_pool, 1)
            eng.wait_ge(setup_pool, 4)
            nc.gpsimd.affine_select(out=p_mask[:, :], in_=p_mask[:, :], compare_op=ALU.is_ge, fill=0.0,
                                    base=0, pattern=[[-DH, HH]], channel_multiplier=1).then_inc(setup_pool, 1)
            row = [[2 * P - GROW, 2], [P, PAIRS], [-KEYS, GH]]
            nc.gpsimd.affine_select(out=v_mask[:, :, :, :], in_=v_mask[:, :, :, :], compare_op=ALU.is_ge, fill=0.0,
                                    base=0, pattern=row, channel_multiplier=1).then_inc(setup_pool, 1)
            eng.wait_ge(setup_pool, 6)
            nc.gpsimd.affine_select(out=p_mask[:, :], in_=p_mask[:, :], compare_op=ALU.is_ge, fill=0.0,
                                    base=DH - 1, pattern=[[DH, HH]], channel_multiplier=-1).then_inc(setup_pool, 1)
            nc.gpsimd.affine_select(out=v_mask[:, :, :, :], in_=v_mask[:, :, :, :], compare_op=ALU.is_ge, fill=0.0,
                                    base=KEYS - 1, pattern=[[-s, n] for s, n in row],
                                    channel_multiplier=-1).then_inc(setup_pool, 1)
            eng.wait_ge(setup_pool, 8)
            nc.gpsimd.tensor_tensor(k_mask[:, :], p_mask[:, 0:GH], p_mask[:, GH:HH], ALU.add).then_inc(setup_pool, 1)
            for gg in range(2):
                _, den = group_part(gg)
                for a in (HI, LO):
                    dst = v_cur[:, gg, :, a, den].rearrange("p j (h d) -> p j h d", d=DH)
                    mask = v_mask[:, gg, :, :].unsqueeze(3).broadcast_to([P, PAIRS, GH, DH])
                    nc.gpsimd.tensor_scalar(dst, mask, 1.0 if a == HI else 0.0, 0.0, ALU.mult, ALU.add)
            eng.wait_ge(setup_pool, 9)
            eng.wait_ge(setup_dve, 6)
            keys(0)
            eng.wait_ge(bias_loaded, 32)
            eng.wait_ge(x_loaded, 16)
            plus_row(xb, x_sb, bo_bc).then_inc(xb_done, 1)
            eng.wait_ge(setup_dve, 7)
            values(0)

            step(0, False, True, False)
            eng.wait_ge(ffn_bias_loaded, 32)
            step(1, True, True, False)
            with eng.Fori(2, NBLK - 1) as i:
                step(i, True, True, True)
            step(NBLK - 1, True, False, True)
            eng.wait_ge(out_stored, 32 * (NBLK - 1))
            x2_plus_bias(NBLK - 1)
            for k in range(FC):
                hidden_low(NBLK - 1, k)


_INS = ["x", "ctx_1024", "L0_xattn_Wq", "L0_xattn_bq", "L0_xattn_Wk", "L0_xattn_bk", "L0_xattn_Wv",
        "L0_xattn_bv", "L0_xattn_Wo", "L0_xattn_bo", "L0_ffn_W1", "L0_ffn_b1", "L0_ffn_W2", "L0_ffn_b2"]


def kernel(**inputs):
    import numpy as _np
    import concourse.bacc as _bacc
    from concourse import mybir as _mybir
    from concourse.bass_utils import run_bass_kernel_spmd as _run

    nc = _bacc.Bacc("TRN2", target_bir_lowering=False, num_devices=1)
    arrays, args = {}, []
    for name in _INS:
        a = _np.ascontiguousarray(inputs[name])
        arrays[f"in_{name}_dram"] = a
        args.append(nc.dram_tensor(f"in_{name}_dram", a.shape, _mybir.dt.from_np(a.dtype), kind="ExternalInput").ap())
    out = nc.dram_tensor("out_dram", (NB, SEQ, D), F32, kind="ExternalOutput").ap()
    xattn_ffn(nc, *args, out)
    r = _run(nc, [arrays], core_ids=[0])
    return r.results[0]["out_dram"]
```

```python
import concourse.bass as bass
from concourse import mybir
from contextlib import ExitStack

F32 = mybir.dt.float32
F32R = mybir.dt.float32r
ALU = mybir.AluOpType
ACT = mybir.ActivationFunctionType
AX = mybir.AxisListType

P = 128
NB, SEQ, D = 4, 1024, 256
KEYS = 77
HEADS, DH = 16, 16
FF = 1024
BLK = 512
NT = BLK // P
NBLK = NB * SEQ // BLK
BLK_PER_B = SEQ // BLK
KC = D // P
FC = FF // P
HH = P // DH
HALVES = HEADS // HH
GH = HH // 2
SROW = HH * KEYS
GROUPS = HEADS // GH
GD = GH * DH
GROW = GH * KEYS
PC = -(-SROW // P)
PW = PC * P
PAIRS = 3
UNITS = HALVES * NT
SCALE = float(DH) ** -0.5
EPS = 1e-5
HI, LO = 0, 1
POOL_UNITS = (0, 3)
POOL_UNITS_0 = tuple(range(UNITS - 1))
POOL_HIDDEN = (2, 5)
STAT_UNITS_0, STAT_UNITS = (7, 7, 7, 7), (1, 2, 4, 5)
WARM_CTX, WARM_NORM, WARM_SCORES, WARM_ROWS, WARM_ROWS2 = 9, 6, 5, 2, 16
PASSES = ((HI, HI), (LO, HI), (HI, LO))


def xattn_ffn(nc, x, ctx, Wq, bq, Wk, bk, Wv, bv, Wo, bo, W1, b1, W2, b2, out):
    x_blk = x.rearrange("b (c t p) d -> (b c) p t d", t=NT, p=P)
    out_blk = out.rearrange("b (c t p) d -> (b c) p t d", t=NT, p=P)
    stack = ExitStack()

    def sb(name, shape, dt=F32):
        return stack.enter_context(nc.sbuf_tensor(name, shape, dt))

    def sem(name):
        return stack.enter_context(nc.semaphore(name))

    def f(ap):
        return ap.bitcast(F32)

    with stack:
        ident = sb("ident", [P, P])
        wq = sb("wq", [P, 2, KC, D], F32R)
        wo = sb("wo", [P, 2, KC, D], F32R)
        w1 = sb("w1", [P, 2, KC, FF], F32R)
        w2 = sb("w2", [P, 2, FC, D], F32R)
        bq_sb = sb("bq_sb", [GD, GROUPS])
        b1_sb = sb("b1_sb", [P, FC])
        bk_sb = sb("bk_sb", [P, 1])
        bo_bc = sb("bo_bc", [P, D])
        b2_bc = sb("b2_bc", [P, D])
        bv_bc = sb("bv_bc", [KEYS, DH])
        eps_sb = sb("eps_sb", [P, 1])
        zero_sb = sb("zero_sb", [P, 1])
        k_rep = sb("k_rep", [P, 2, NB * KEYS])
        v_rows = sb("v_rows", [P, PC, 2, NB, DH])
        p_mask = sb("p_mask", [P, HH])
        k_mask = sb("k_mask", [P, GH])
        v_mask = sb("v_mask", [P, 2, PAIRS, GH])
        k_cur = sb("k_cur", [P, 2, GH, KEYS], F32R)
        v_cur = sb("v_cur", [P, 2, PAIRS, 2, P], F32R)
        x_sb = sb("x_sb", [P, NT, D])
        xb = sb("xb", [P, NT, D])
        xn = sb("xn", [P, NT, D])
        xnT = sb("xnT", [P, 2, KC, BLK], F32R)
        qT = sb("qT", [P, GROUPS, BLK], F32R)
        s_sub = sb("s_sub", [P, 2, PW])
        e_f = sb("e_f", [P, 2, PW])
        pT = sb("pT", [P, 2, HALVES, PC, BLK], F32R)
        att = sb("att", [P, HALVES, BLK])
        attT = sb("attT", [P, 2, HALVES, BLK], F32R)
        smax = sb("smax", [P, 2, HH])
        x2 = sb("x2", [P, NT, D])
        x2b = sb("x2b", [P, NT, D])
        xn2 = sb("xn2", [P, NT, D])
        x2nT = sb("x2nT", [P, 2, KC, BLK], F32R)
        h_f = sb("h_f", [P, 2, BLK])
        st = [sb(f"st{n}", [P, NT, 6]) for n in (1, 2)]
        mv = [sb(f"mv{n}", [P, NT, 2]) for n in (1, 2)]
        nmean = [sb(f"nmean{n}", [P, NT]) for n in (1, 2)]
        lnv = [sb(f"lnv{n}", [P, NT]) for n in (1, 2)]
        rstd = [sb(f"rstd{n}", [P, NT]) for n in (1, 2)]
        y2 = [sb(f"y2_{n}", [P, NT]) for n in (1, 2)]
        vy2 = [sb(f"vy2_{n}", [P, NT]) for n in (1, 2)]
        corr = [sb(f"corr{n}", [P, NT]) for n in (1, 2)]
        istd = [sb(f"istd{n}", [P, NT]) for n in (1, 2)]
        count2 = sb("count2", [P, NT])
        with ExitStack() as early:
            def tmp(name, shape):
                return early.enter_context(nc.sbuf_tensor(name, shape, F32))
            w1_raw = tmp("w1_raw", [P, KC, FF])
            w2_raw = tmp("w2_raw", [P, FC, D])
            wo_raw = tmp("wo_raw", [P, KC, D])
            wq_raw = tmp("wq_raw", [P, KC, D])
            ctx_sb = tmp("ctx_sb", [KEYS, NB, D])
            ctxT = tmp("ctxT", [P, KC, NB * KEYS])
            wk_raw = tmp("wk_raw", [P, KC, DH])
            wk_rep = tmp("wk_rep", [P, KC, HH, DH])
            wv_sb = tmp("wv_sb", [P, KC, DH])
            v_f = tmp("v_f", [KEYS, NB, DH])
            v_all = tmp("v_all", [KEYS, 2, NB, DH])
        hT = sb("hT", [P, 2, FC, BLK], F32R)
        sel = x2b[0:KEYS, :, :].rearrange("k t d -> k (t d)")[:, 0:PW]

        s_ps = stack.enter_context(nc.psum_tensor("s_ps", [P, 4, 512], F32))
        t_ps = stack.enter_context(nc.psum_tensor("t_ps", [P, 2, 512], F32))
        g_ps = stack.enter_context(nc.psum_tensor("g_ps", [P, 2, 512], F32))

        def subT(ffn, k):
            ps = t_ps if ffn or k % 2 == 0 else g_ps
            return ps[:, :, :].rearrange("p a b -> p (a b)")[:, 0:PW]

        kv_loaded, wk_loaded = sem("kv_loaded"), sem("wk_loaded")
        kv_bias_loaded, bias_loaded, ffn_bias_loaded = sem("kv_bias_loaded"), sem("bias_loaded"), sem("ffn_bias_loaded")
        wq_loaded, wo_loaded = sem("wq_loaded"), sem("wo_loaded")
        w1_loaded, w2_loaded = sem("w1_loaded"), sem("w2_loaded")
        x_loaded, out_stored = sem("x_loaded"), sem("out_stored")
        setup_pool, setup_dve, setup_act, setup_pe = (sem(f"setup_{e}") for e in ("pool", "dve", "act", "pe"))
        x_half_loaded = sem("x_half_loaded")
        wk_repeated, v_rows_made = sem("wk_repeated"), sem("v_rows_made")
        w_hi, w_lo, w_lo_pool = sem("w_hi"), sem("w_lo"), sem("w_lo_pool")
        stats_done = [sem(f"stats{n}_done") for n in (1, 2)]
        aggr_done = [sem(f"aggr{n}_done") for n in (1, 2)]
        nmean_done = [sem(f"nmean{n}_done") for n in (1, 2)]
        lnv_done = [sem(f"lnv{n}_done") for n in (1, 2)]
        rstd_done = [sem(f"rstd{n}_done") for n in (1, 2)]
        refined = [sem(f"refined{n}") for n in (1, 2)]
        xn_done, xn2_done = sem("xn_done"), sem("xn2_done")
        xb_done, x2b_done = sem("xb_done"), sem("x2b_done")
        xnT_ps, xnT_hi, xnT_lo = sem("xnT_ps"), sem("xnT_hi"), sem("xnT_lo")
        q_ps, q_hi, q_lo = sem("q_ps"), sem("q_hi"), sem("q_lo")
        k_ready, v_ready = sem("k_ready"), sem("v_ready")
        score_ps, max_done, sub_done = sem("score_ps"), sem("max_done"), sem("sub_done")
        subT_ps, p_hi, e_done = sem("subT_ps"), sem("p_hi"), sem("e_done")
        p_lo, p_lo_pool = sem("p_lo"), sem("p_lo_pool")
        pv_ps, log_done, inv_done, att_done = sem("pv_ps"), sem("log_done"), sem("inv_done"), sem("att_done")
        att_hi, att_lo = sem("att_hi"), sem("att_lo")
        o_ps, x2_done = sem("o_ps"), sem("x2_done")
        x2nT_ps, x2nT_hi, x2nT_lo = sem("x2nT_ps"), sem("x2nT_hi"), sem("x2nT_lo")
        h_ps, h_hi, hf_done, h_lo = sem("h_ps"), sem("h_hi"), sem("hf_done"), sem("h_lo")
        h_hi_pool = sem("h_hi_pool")
        y_ps, out_done = sem("y_ps"), sem("out_done")

        block = stack.enter_context(nc.Block())

        w1_pieces = [(w1_raw[:, c, h * 512:(h + 1) * 512], w1[:, HI, c, h * 512:(h + 1) * 512],
                      w1[:, LO, c, h * 512:(h + 1) * 512], w1_loaded) for c in range(KC) for h in range(2)]
        w2_pieces = [(w2_raw[:, c:c + 2, :], w2[:, HI, c:c + 2, :], w2[:, LO, c:c + 2, :], w2_loaded)
                     for c in range(0, FC, 2)]
        pieces = w1_pieces + w2_pieces
        EARLY_PIECES = len(pieces) - UNITS // 2

        def group_part(g):
            a = (g % 2) * 64
            return slice(a, a + 64), slice(64 - a, 128 - a)

        def pool_units(i):
            return POOL_UNITS_0 if isinstance(i, int) and i == 0 else POOL_UNITS

        def prob_low_done(i, k):
            units = pool_units(i)
            before = sum(u < k for u in units)
            more = 0 if isinstance(i, int) and i == 0 else len(POOL_UNITS_0) - len(POOL_UNITS)
            if k in units:
                return p_lo_pool, len(units) * i + before + 1 + more
            return p_lo, (UNITS - len(units)) * i + k - before + 1 - more

        def rows_after(ffn):
            return 2 if ffn else 1

        def values_bank(g):
            return 3 - g

        def query_bank(m):
            return 3 - m

        @block.sync
        def _(eng):
            eng.dma_start(x_sb[:, 0:2, :], x_blk[0][:, 0:2, :]).then_inc(x_half_loaded, 16)
            eng.dma_start(x_sb[:, 2:4, :], x_blk[0][:, 2:4, :]).then_inc(x_loaded, 16)
            eng.dma_start(ctx_sb[:, :, :], ctx.rearrange("b k d -> k b d")).then_inc(kv_loaded, 16)
            eng.dma_start(wq_raw[:, :, :], Wq.rearrange("(c p) n -> p c n", p=P)).then_inc(wq_loaded, 16)
            for h in range(HH):
                eng.dma_start(bk_sb[h * DH:(h + 1) * DH, :], bk.rearrange("(d a) -> d a", a=1)).then_inc(kv_bias_loaded, 16)
            eng.dma_start(bv_bc[:, :], bv.partition_broadcast(KEYS)).then_inc(kv_bias_loaded, 16)
            eng.dma_start(bq_sb[:, :], bq.rearrange("(g p) -> p g", p=GD), allow_slow_non_contiguous=True).then_inc(bias_loaded, 16)
            eng.dma_start(bo_bc[:, :], bo.partition_broadcast(P)).then_inc(bias_loaded, 16)
            eng.dma_start(wo_raw[:, :, :], Wo.rearrange("(c p) n -> p c n", p=P)).then_inc(wo_loaded, 16)
            eng.dma_start(w1_raw[:, :, :], W1.rearrange("(c p) n -> p c n", p=P)).then_inc(w1_loaded, 16)
            eng.dma_start(w2_raw[:, :, :], W2.rearrange("(c p) n -> p c n", p=P)).then_inc(w2_loaded, 16)
            eng.dma_start(b1_sb[:, :], b1.rearrange("(m p) -> p m", p=P), allow_slow_non_contiguous=True).then_inc(ffn_bias_loaded, 16)
            eng.dma_start(b2_bc[:, :], b2.partition_broadcast(P)).then_inc(ffn_bias_loaded, 16)

            def load_next(i):
                eng.wait_ge(xb_done, i + 1)
                eng.dma_start(x_sb[:, :, :], x_blk[i + 1]).then_inc(x_loaded, 16)

            def store(i, tp):
                eng.wait_ge(out_done, 2 * i + tp + 1)
                eng.dma_start(out_blk[i][:, 2 * tp:2 * tp + 2, :],
                              x2b[:, 2 * tp:2 * tp + 2, :]).then_inc(out_stored, 16)

            load_next(0)
            load_next(1)
            store(0, 0)
            with eng.Fori(2, NBLK - 1) as i:
                load_next(i)
                store(i - 2, 1)
                store(i - 1, 0)
            store(NBLK - 3, 1)
            store(NBLK - 2, 0)
            store(NBLK - 2, 1)
            for t in range(NT):
                eng.wait_ge(out_done, 2 * (NBLK - 1) + t + 1)
                eng.dma_start(out_blk[NBLK - 1][:, t, :], x2b[:, t, :]).then_inc(out_stored, 16)
            eng.wait_ge(out_stored, 32 * (NBLK - 1) + 16 * NT)

        @block.tensor
        def _(eng):
            def mm3(o, lhs, rhs, steps):
                n = len(steps) * len(PASSES)
                j = 0
                for s in steps:
                    for a, b in PASSES:
                        last = nc.tensor.matmul(o, lhs(a, s), rhs(b, s), start=(j == 0), stop=(j == n - 1))
                        j += 1
                return last

            def transpose_rows(src, src_done, done, i):
                for t in range(NT):
                    eng.wait_ge(src_done, 4 * i + t + 1)
                    for c in range(KC):
                        tr = nc.tensor.transpose(t_ps[:, c, t * P:(t + 1) * P],
                                                 src[:, t, c * P:(c + 1) * P], ident[:, :])
                        if t == NT - 1:
                            tr.then_inc(done, 1)

            def queries():
                for m in range(KC):
                    mm3(s_ps[:, query_bank(m), :], lambda a, c: wq[:, a, c, m * P:(m + 1) * P],
                        lambda b, c: xnT[:, b, c, :], range(KC)).then_inc(q_ps, 1)

            def scores(u):
                hf, t = divmod(u, NT)
                for j in range(2):
                    for a in (HI, LO):
                        last = nc.tensor.matmul(s_ps[:, 2 * (u % 2) + j, 0:GROW],
                                                qT[:, 2 * hf + j, t * P:(t + 1) * P],
                                                k_cur[:, a, :, :].rearrange("p h k -> p (h k)"),
                                                start=(a == HI), stop=(a == LO))
                last.then_inc(score_ps, 1)

            def ffn_in(i, k, ffn_before=True):
                if k == 1 and ffn_before:
                    eng.wait_ge(out_done, 2 * i)
                if k >= 2:
                    eng.wait_ge(hf_done, 8 * i + k - 1)

                def rows(b, c):
                    if k == 0 and b == HI:
                        eng.wait_ge(x2nT_lo, 2 * i + c + 1)
                    return x2nT[:, b, c, :]

                mm3(g_ps[:, k % 2, :], lambda a, c: w1[:, a, c, k * P:(k + 1) * P],
                    rows, range(KC)).then_inc(h_ps, 1)

            def ffn_out(t, out=None, waits=None):
                def hidden_rows(a, k):
                    if waits is not None and a == HI:
                        eng.wait_ge(h_lo, waits + k + 1)
                    return hT[:, a, k, t * P:(t + 1) * P]

                if out is None:
                    out = g_ps[:, t // 2, (t % 2) * D:(t % 2 + 1) * D]
                mm3(out, hidden_rows,
                    lambda b, k: w2[:, b, k, :], range(FC)).then_inc(y_ps, 1)

            def transpose_unit(i, k, ffn):
                eng.wait_ge(sub_done, 8 * i + k + 1)
                if ffn and k >= 1:
                    eng.wait_ge(e_done, 8 * i + k)
                if not ffn and k >= 2:
                    eng.wait_ge(e_done, 8 * i + k - 1)
                if not ffn and k == 1:
                    eng.wait_ge(v_rows_made, 1)
                for c in range(PC):
                    last = nc.tensor.transpose(subT(ffn, k)[:, c * P:(c + 1) * P],
                                               s_sub[:, k % 2, c * P:(c + 1) * P], ident[:, :])
                last.then_inc(subT_ps, 1)
                if k + 2 < UNITS:
                    scores(k + 2)

            def step(i, ffn, more, ffn_before=True):
                if ffn and not ffn_before:
                    eng.wait_ge(w_lo_pool, 1 + len(pieces))
                for k in range(UNITS):
                    if ffn:
                        ffn_in(i - 1, k, ffn_before)
                    transpose_unit(i, k, ffn)
                eng.wait_ge(v_ready, i + 1)
                for g in range(4):
                    hf, gg = divmod(g, 2)
                    if gg == 0:
                        for pool in (False, True):
                            units = [u for u in range(NT * (hf + 1)) if (u in pool_units(i)) == pool]
                            if units:
                                eng.wait_ge(*prob_low_done(i, units[-1]))
                    mm3(s_ps[:, values_bank(g), :], lambda a, j: v_cur[:, gg, j, a, :],
                        lambda b, j: pT[:, b, hf, 2 * gg + j, :], range(PAIRS)).then_inc(pv_ps, 1)
                    if more and g == rows_after(ffn):
                        transpose_rows(xn, xn_done, xnT_ps, i + 1)
                if not ffn:
                    keep_warm(WARM_ROWS)
                    eng.wait_ge(xnT_lo, 2 * (i + 2))
                    eng.wait_ge(att_done, 4 * i + 2)
                    queries()
                    eng.wait_ge(w_lo_pool, 1)
                else:
                    eng.wait_ge(h_lo, 8 * i)
                    ffn_out(0)
                    if more:
                        ffn_out(1)
                        eng.wait_ge(xnT_lo, 2 * (i + 2))
                eng.wait_ge(att_lo, 2 * (i + 1))
                for tp in range(2):
                    for t in (2 * tp, 2 * tp + 1):
                        last = mm3(t_ps[:, tp, (t % 2) * D:(t % 2 + 1) * D],
                                   lambda a, c: attT[:, a, c, t * P:(t + 1) * P],
                                   lambda b, c: wo[:, b, c, :], range(KC))
                    last.then_inc(o_ps, 1)
                if not ffn:
                    scores_0(i + 1)
                    keep_warm(WARM_ROWS2)
                elif more:
                    queries()
                    ffn_out(2)
                else:
                    ffn_out(1)
                    ffn_out(2)
                transpose_rows(xn2, xn2_done, x2nT_ps, i)
                if ffn and more:
                    scores_0(i + 1)
                if ffn:
                    ffn_out(3)
                if more:
                    scores_1(i + 1)

            def scores_0(i):
                eng.wait_ge(q_lo, GROUPS * i + 2)
                eng.wait_ge(k_ready, i + 1)
                scores(0)

            def scores_1(i):
                eng.wait_ge(q_lo, GROUPS * (i + 1))
                scores(1)

            def keep_warm(n, ps=g_ps):
                for _ in range(n):
                    nc.tensor.matmul(ps[:, 1, 0:P], ident[:, :], ident[:, :], start=True, stop=True)

            eng.wait_ge(setup_pool, 2)
            keep_warm(WARM_CTX)
            eng.wait_ge(kv_loaded, 16)
            for c in range(KC):
                for b in range(NB):
                    last = nc.tensor.transpose(s_ps[:, c, b * KEYS:(b + 1) * KEYS],
                                               ctx_sb[:, b, c * P:(c + 1) * P], ident[0:KEYS, 0:KEYS])
            last.then_inc(setup_pe, 1)
            keep_warm(WARM_NORM)
            transpose_rows(xn, xn_done, xnT_ps, 0)
            eng.wait_ge(setup_act, 1)
            eng.wait_ge(setup_dve, 1)
            eng.wait_ge(wk_repeated, 1)
            for c in range(KC):
                last = nc.tensor.matmul(s_ps[:, 0, 0:NB * KEYS], wk_rep[:, c, :, :].rearrange("p h d -> p (h d)"),
                                        ctxT[:, c, :], start=(c == 0), stop=(c == KC - 1))
            last.then_inc(setup_pe, 1)
            for b in range(NB):
                for c in range(KC):
                    last = nc.tensor.matmul(s_ps[0:KEYS, 1, b * DH:(b + 1) * DH],
                                            ctxT[:, c, b * KEYS:(b + 1) * KEYS], wv_sb[:, c, :],
                                            start=(c == 0), stop=(c == KC - 1))
            last.then_inc(setup_pe, 1)
            eng.wait_ge(xnT_lo, 2)
            eng.wait_ge(w_lo, 1)
            queries()
            eng.wait_ge(setup_dve, 5)
            eng.wait_ge(setup_pool, 4)
            for c in range(PC):
                last = nc.tensor.matmul(g_ps[:, c // 4, (c % 4) * P:(c % 4 + 1) * P],
                                        sel[:, c * P:(c + 1) * P],
                                        v_all[:, :, :, :].rearrange("k a b d -> k (a b d)"),
                                        start=True, stop=True)
            last.then_inc(setup_pe, 1)
            scores_0(0)
            scores_1(0)
            keep_warm(WARM_SCORES, t_ps)

            step(0, False, True)
            step(1, True, True, False)
            with eng.Fori(2, NBLK - 1) as i:
                step(i, True, True)
            step(NBLK - 1, True, False)
            for k in range(FC):
                ffn_in(NBLK - 1, k)
            for t in range(NT):
                ffn_out(t, s_ps[:, t, 0:D], 8 * (NBLK - 1) if t == 0 else None)

        @block.scalar
        def _(eng):
            eng.dma_start(wk_raw[:, :, :], Wk.rearrange("(c p) n -> p c n", p=P)).then_inc(wk_loaded, 16)
            eng.dma_start(wv_sb[:, :, :], Wv.rearrange("(c p) n -> p c n", p=P)).then_inc(wk_loaded, 16)
            eng.preload_act_table_set("natural_log_exp_and_others")

            def inv_std(n, i):
                eng.wait_ge(nmean_done[n], i + 1)
                nc.scalar.activation(lnv[n][:, :], mv[n][:, :, 1], ACT.Ln, bias=eps_sb[:, :]).then_inc(lnv_done[n], 1)
                eng.wait_ge(lnv_done[n], i + 1)
                nc.scalar.activation(rstd[n][:, :], lnv[n][:, :], ACT.Exp, scale=-0.5).then_inc(rstd_done[n], 1)

            def rows_high(dst, ps_done, done, i):
                for c in range(KC):
                    eng.wait_ge(ps_done, 2 * i + c + 1)
                    nc.scalar.activation(dst[:, HI, c, :], t_ps[:, c, :], ACT.Copy).then_inc(done, 1)

            def query_high(i, m):
                eng.wait_ge(q_ps, 2 * i + m + 1)
                for j in range(2):
                    nc.scalar.activation(qT[0:GD, 2 * m + j, :], s_ps[j * GD:(j + 1) * GD, query_bank(m), :], ACT.Identity,
                                         bias=bq_sb[:, 2 * m + j:2 * m + j + 1]).then_inc(q_hi, 1)

            def hidden(i, k, pool_makes=POOL_HIDDEN):
                eng.wait_ge(h_ps, 8 * i + k + 1)
                if k not in pool_makes:
                    nc.scalar.activation(hT[:, HI, k, :], g_ps[:, k % 2, :], ACT.Relu,
                                         bias=b1_sb[:, k:k + 1]).then_inc(h_hi, 1)
                if k >= 2:
                    eng.wait_ge(h_lo, 8 * i + k - 1)
                nc.scalar.activation(h_f[:, k % 2, :], g_ps[:, k % 2, :], ACT.Relu,
                                     bias=b1_sb[:, k:k + 1]).then_inc(hf_done, 1)

            def step(i, ffn, more):
                for k in range(UNITS):
                    hf, t = divmod(k, NT)
                    eng.wait_ge(subT_ps, 8 * i + k + 1)
                    src = subT(ffn, k).rearrange("p (c t) -> p c t", t=P)
                    nc.scalar.activation(pT[:, HI, hf, :, t * P:(t + 1) * P], src, ACT.Exp,
                                         scale=SCALE).then_inc(p_hi, 1)
                    if k >= 2:
                        eng.wait_ge(*prob_low_done(i, k - 2))
                    nc.scalar.activation(e_f[:, k % 2, :], subT(ffn, k), ACT.Exp,
                                         scale=SCALE).then_inc(e_done, 1)
                    if ffn:
                        hidden(i - 1, k)
                    elif k % 2 == 1:
                        weight_high(EARLY_PIECES + k // 2)
                if more:
                    inv_std(0, i + 1)
                for g in range(4):
                    num, den = group_part(g)
                    hf = g // 2
                    eng.wait_ge(pv_ps, 4 * i + g + 1)
                    nc.scalar.activation(att[num, hf, :], s_ps[den, values_bank(g), :], ACT.Ln).then_inc(log_done, 1)
                    eng.wait_ge(log_done, 4 * i + g + 1)
                    nc.scalar.activation(att[num, hf, :], att[num, hf, :], ACT.Exp, scale=-1.0).then_inc(inv_done, 1)
                    if g == 2:
                        att_high(i, 0)
                    if more and g == rows_after(ffn):
                        rows_high(xnT, xnT_ps, xnT_hi, i + 1)
                att_high(i, 1)
                if more:
                    query_high(i + 1, 0)
                if more and not ffn:
                    query_high(i + 1, 1)
                inv_std(1, i)
                if more and ffn:
                    query_high(i + 1, 1)
                rows_high(x2nT, x2nT_ps, x2nT_hi, i)

            def weight_high(k):
                raw, high, _, loaded = pieces[k]
                eng.wait_ge(loaded, 16)
                nc.scalar.activation(high, raw, ACT.Copy).then_inc(w_hi, 1)

            def att_high(i, hf):
                eng.wait_ge(att_done, 4 * i + 2 * hf + 2)
                nc.scalar.activation(attT[:, HI, hf, :], att[:, hf, :], ACT.Copy).then_inc(att_hi, 1)

            eng.wait_ge(setup_dve, 1)
            inv_std(0, 0)
            eng.wait_ge(setup_pe, 1)
            nc.scalar.activation(ctxT[:, :, :], s_ps[:, 0:KC, 0:NB * KEYS], ACT.Copy).then_inc(setup_act, 1)
            eng.wait_ge(wq_loaded, 16)
            nc.scalar.activation(wq[:, HI, :, :], wq_raw[:, :, :], ACT.Copy).then_inc(w_hi, 1)
            rows_high(xnT, xnT_ps, xnT_hi, 0)
            eng.wait_ge(kv_bias_loaded, 16 * (HH + 1))
            eng.wait_ge(setup_pe, 2)
            nc.scalar.activation(k_rep[:, HI, :].bitcast(F32R), s_ps[:, 0, 0:NB * KEYS], ACT.Identity,
                                 bias=bk_sb[:, :]).then_inc(setup_act, 1)
            eng.wait_ge(wo_loaded, 16)
            nc.scalar.activation(wo[:, HI, :, :], wo_raw[:, :, :], ACT.Copy).then_inc(w_hi, 1)
            eng.wait_ge(bias_loaded, 32)
            query_high(0, 0)
            query_high(0, 1)
            eng.wait_ge(setup_pe, 4)
            nc.scalar.activation(v_rows[:, 0:4, :, :, :].rearrange("p c a b d -> p (c a b d)"),
                                 g_ps[:, 0, :], ACT.Copy)
            nc.scalar.activation(v_rows[:, 4, :, :, :].rearrange("p a b d -> p (a b d)"),
                                 g_ps[:, 1, 0:P], ACT.Copy).then_inc(v_rows_made, 1)
            for k in range(EARLY_PIECES):
                weight_high(k)

            step(0, False, True)
            eng.wait_ge(ffn_bias_loaded, 32)
            step(1, True, True)
            with eng.Fori(2, NBLK - 1) as i:
                step(i, True, True)
            step(NBLK - 1, True, False)
            for k in range(FC):
                hidden(NBLK - 1, k, ())

        @block.vector
        def _(eng):
            def stats(n, src, i, tiles):
                for t in tiles:
                    nc.vector.bn_stats(st[n][:, t, :], src[:, t, :]).then_inc(stats_done[n], 1)

            def moments(n, i):
                for t in range(NT):
                    nc.vector.bn_aggr(mv[n][:, t, :], st[n][:, t, :]).then_inc(aggr_done[n], 1)
                eng.wait_ge(aggr_done[n], 4 * (i + 1))
                nc.vector.tensor_scalar(nmean[n][:, :], mv[n][:, :, 0], -1.0, None, ALU.mult).then_inc(nmean_done[n], 1)

            def normed(n, dst, src, done, i):
                eng.wait_ge(rstd_done[n], i + 1)
                nc.vector.tensor_tensor(y2[n][:, :], rstd[n][:, :], rstd[n][:, :], ALU.mult).then_inc(refined[n], 1)
                eng.wait_ge(refined[n], 4 * i + 1)
                nc.vector.scalar_tensor_tensor(vy2[n][:, :], mv[n][:, :, 1], EPS, y2[n][:, :],
                                               ALU.add, ALU.mult).then_inc(refined[n], 1)
                eng.wait_ge(refined[n], 4 * i + 2)
                nc.vector.tensor_scalar(corr[n][:, :], vy2[n][:, :], -0.5, 1.5, ALU.mult, ALU.add).then_inc(refined[n], 1)
                eng.wait_ge(refined[n], 4 * i + 3)
                nc.vector.tensor_tensor(istd[n][:, :], rstd[n][:, :], corr[n][:, :], ALU.mult).then_inc(refined[n], 1)
                eng.wait_ge(refined[n], 4 * i + 4)
                for t in range(NT):
                    nc.vector.tensor_scalar(dst[:, t, :], src[:, t, :], nmean[n][:, t:t + 1],
                                            istd[n][:, t:t + 1], ALU.add, ALU.mult).then_inc(done, 1)

            def rows_low(dst, high_done, done, i):
                for c in range(KC):
                    eng.wait_ge(high_done, 2 * i + c + 1)
                    nc.vector.tensor_tensor(dst[:, LO, c, :], t_ps[:, c, :], f(dst[:, HI, c, :]),
                                            ALU.subtract).then_inc(done, 1)

            def query_low(i, groups):
                for g in groups:
                    m, j = divmod(g, 2)
                    eng.wait_ge(q_hi, GROUPS * i + g + 1)
                    nc.vector.scalar_tensor_tensor(qT[GD:P, g, :], s_ps[j * GD:(j + 1) * GD, query_bank(m), :],
                                                   bq_sb[:, g:g + 1], f(qT[0:GD, g, :]),
                                                   ALU.add, ALU.subtract).then_inc(q_lo, 1)

            def prob_low(i, k):
                if k in pool_units(i):
                    return
                hf, t = divmod(k, NT)
                eng.wait_ge(e_done, 8 * i + k + 1)
                nc.vector.tensor_tensor(pT[:, LO, hf, :, t * P:(t + 1) * P],
                                        e_f[:, k % 2, :].rearrange("p (c t) -> p c t", t=P),
                                        f(pT[:, HI, hf, :, t * P:(t + 1) * P]), ALU.subtract).then_inc(p_lo, 1)

            def att_low(i, hf):
                eng.wait_ge(att_hi, 2 * i + hf + 1)
                nc.vector.tensor_tensor(attT[:, LO, hf, :], att[:, hf, :], f(attT[:, HI, hf, :]),
                                        ALU.subtract).then_inc(att_lo, 1)

            def result(i, tp):
                eng.wait_ge(y_ps, 4 * i + 2 * tp + 2)
                nc.vector.tensor_tensor(x2b[:, 2 * tp:2 * tp + 2, :],
                                        g_ps[:, tp, :].rearrange("p (t d) -> p t d", d=D),
                                        x2b[:, 2 * tp:2 * tp + 2, :], ALU.add).then_inc(out_done, 1)

            def scores_of(k):
                return s_ps[:, 2 * (k % 2):2 * (k % 2) + 2, 0:GROW].rearrange("p j (h k) -> p j h k", k=KEYS)

            def max_of(k):
                return smax[:, k % 2, :].rearrange("p (j h) -> p j h", j=2)

            def maximum(i, k):
                eng.wait_ge(score_ps, 8 * i + k + 1)
                nc.vector.tensor_reduce(max_of(k), scores_of(k), AX.X, ALU.max).then_inc(max_done, 1)

            def minus_maximum(i, k):
                eng.wait_ge(max_done, 8 * i + k + 1)
                nc.vector.tensor_tensor(s_sub[:, k % 2, 0:SROW].rearrange("p (j h k) -> p j h k", j=2, k=KEYS),
                                        scores_of(k), max_of(k).unsqueeze(3).broadcast_to([P, 2, GH, KEYS]),
                                        ALU.subtract).then_inc(sub_done, 1)

            def step(i, ffn, more):
                stat_units = STAT_UNITS if ffn else STAT_UNITS_0
                for k in range(UNITS):
                    if k > 0:
                        maximum(i, k)
                    if more and ffn and k == 7:
                        eng.wait_ge(stats_done[0], 4 * (i + 2))
                    if k >= 2:
                        prob_low(i, k - 2)
                        eng.wait_ge(subT_ps, 8 * i + k - 1)
                    if k > 0:
                        minus_maximum(i, k)
                    if more and k in stat_units:
                        if k == stat_units[0]:
                            eng.wait_ge(x_loaded, 16 * (i + 2))
                        stats(0, x_sb, i + 1, [t for t in range(NT) if stat_units[t] == k])
                    if not ffn and k == 7:
                        eng.wait_ge(stats_done[0], 4 * (i + 2))
                    if more and k == 7:
                        moments(0, i + 1)
                prob_low(i, UNITS - 2)
                prob_low(i, UNITS - 1)
                if more:
                    normed(0, xn, x_sb, xn_done, i + 1)
                for g in range(4):
                    num, _ = group_part(g)
                    eng.wait_ge(inv_done, 4 * i + g + 1)
                    nc.vector.tensor_tensor(att[num, g // 2, :], s_ps[num, values_bank(g), :], att[num, g // 2, :],
                                            ALU.mult).then_inc(att_done, 1)
                    if g == 2:
                        att_low(i, 0)
                    if more and g == rows_after(ffn):
                        rows_low(xnT, xnT_hi, xnT_lo, i + 1)
                att_low(i, 1)
                if not ffn:
                    query_low(i + 1, (0, 1, 2))
                if ffn:
                    eng.wait_ge(x2b_done, i)
                if more and ffn:
                    result(i - 1, 0)
                for tp in range(2):
                    eng.wait_ge(o_ps, 2 * i + tp + 1)
                    nc.vector.tensor_tensor(x2[:, 2 * tp:2 * tp + 2, :],
                                            t_ps[:, tp, :].rearrange("p (t d) -> p t d", d=D),
                                            xb[:, 2 * tp:2 * tp + 2, :], ALU.add).then_inc(x2_done, 1)
                    eng.wait_ge(x2_done, 2 * i + tp + 1)
                    stats(1, x2, i, (2 * tp, 2 * tp + 1))
                eng.wait_ge(stats_done[1], 4 * (i + 1))
                nc.vector.tensor_scalar(count2[:, :], st[1][:, :, 0], 2.0, None, ALU.mult)
                moments(1, i)
                if more:
                    query_low(i + 1, (0, 1) if ffn else (3,))
                normed(1, xn2, x2, xn2_done, i)
                if not ffn:
                    maximum(i + 1, 0)
                if more and ffn:
                    query_low(i + 1, (2, 3))
                if ffn and not more:
                    result(i - 1, 0)
                rows_low(x2nT, x2nT_hi, x2nT_lo, i)
                if more and ffn:
                    maximum(i + 1, 0)
                if more:
                    minus_maximum(i + 1, 0)
                if ffn:
                    result(i - 1, 1)

            nc.vector.memset(eps_sb[:, :], EPS)
            nc.vector.memset(s_sub[:, :, SROW:PW], 0.0).then_inc(setup_dve, 1)
            eng.wait_ge(x_half_loaded, 16)
            stats(0, x_sb, 0, (0, 1))
            eng.wait_ge(x_loaded, 16)
            stats(0, x_sb, 0, (2, 3))
            eng.wait_ge(stats_done[0], 4)
            moments(0, 0)
            normed(0, xn, x_sb, xn_done, 0)
            eng.wait_ge(w_hi, 1)
            nc.vector.tensor_tensor(wq[:, LO, :, :], wq_raw[:, :, :], f(wq[:, HI, :, :]),
                                    ALU.subtract).then_inc(w_lo, 1)
            rows_low(xnT, xnT_hi, xnT_lo, 0)
            eng.wait_ge(setup_act, 2)
            nc.vector.scalar_tensor_tensor(k_rep[:, LO, :].bitcast(F32R), s_ps[:, 0, 0:NB * KEYS], bk_sb[:, :],
                                           k_rep[:, HI, :], ALU.add, ALU.subtract).then_inc(setup_dve, 1)
            eng.wait_ge(kv_bias_loaded, 16 * (HH + 1))
            eng.wait_ge(setup_pe, 3)
            nc.vector.tensor_tensor(v_f[:, :, :], s_ps[0:KEYS, 1, 0:NB * DH].rearrange("k (b d) -> k b d", d=DH),
                                    bv_bc[:, :].unsqueeze(1).broadcast_to([KEYS, NB, DH]), ALU.add).then_inc(setup_dve, 1)
            eng.wait_ge(setup_dve, 3)
            nc.vector.tensor_copy(v_all[:, HI, :, :].bitcast(F32R), v_f[:, :, :]).then_inc(setup_dve, 1)
            eng.wait_ge(setup_dve, 4)
            nc.vector.tensor_tensor(v_all[:, LO, :, :].bitcast(F32R), v_f[:, :, :], v_all[:, HI, :, :],
                                    ALU.subtract).then_inc(setup_dve, 1)
            eng.wait_ge(bias_loaded, 32)
            query_low(0, range(GROUPS))
            maximum(0, 0)
            minus_maximum(0, 0)
            step(0, False, True)
            step(1, True, True)
            with eng.Fori(2, NBLK - 1) as i:
                step(i, True, True)
            step(NBLK - 1, True, False)
            for k in range(FC):
                eng.wait_ge(hf_done, 8 * (NBLK - 1) + k + 1)
                nc.vector.tensor_tensor(hT[:, LO, k, :], h_f[:, k % 2, :], f(hT[:, HI, k, :]),
                                        ALU.subtract).then_inc(h_lo, 1)
            eng.wait_ge(x2b_done, NBLK)
            for t in range(NT):
                eng.wait_ge(y_ps, 4 * (NBLK - 1) + t + 1)
                nc.vector.tensor_tensor(x2b[:, t, :], s_ps[:, t, 0:D], x2b[:, t, :],
                                        ALU.add).then_inc(out_done, 1)

        @block.gpsimd
        def _(eng):
            def plus_row(dst, src, row):
                return nc.gpsimd.tensor_tensor(dst[:, :, :], src[:, :, :],
                                               row[:, :].unsqueeze(1).broadcast_to([P, NT, D]), ALU.add)

            def keys(i):
                b = i // BLK_PER_B
                for a in (HI, LO):
                    last = nc.gpsimd.tensor_tensor(
                        k_cur[:, a, :, :], k_rep[:, a, bass.ds(b * KEYS, KEYS)].unsqueeze(1).broadcast_to([P, GH, KEYS]),
                        k_mask[:, :].unsqueeze(2).broadcast_to([P, GH, KEYS]), ALU.mult)
                last.then_inc(k_ready, 1)

            def values(i):
                b = i // BLK_PER_B
                for gg in range(2):
                    num, _ = group_part(gg)
                    for a in (HI, LO):
                        last = nc.gpsimd.tensor_tensor(
                            v_cur[:, gg, :, a, num].rearrange("p j (h d) -> p j h d", d=DH),
                            v_rows[:, 2 * gg:2 * gg + PAIRS, a, bass.ds(b, 1), :].broadcast_to([P, PAIRS, GH, DH]),
                            v_mask[:, gg, :, :].unsqueeze(3).broadcast_to([P, PAIRS, GH, DH]), ALU.mult)
                last.then_inc(v_ready, 1)

            def hidden_low(i, k):
                eng.wait_ge(hf_done, 8 * i + k + 1)
                if k in POOL_HIDDEN:
                    nc.gpsimd.tensor_tensor(hT[:, HI, k, :], h_f[:, k % 2, :], zero_sb[:, :].broadcast_to([P, BLK]),
                                            ALU.add).then_inc(h_hi_pool, 1)
                    eng.wait_ge(h_hi_pool, len(POOL_HIDDEN) * i + POOL_HIDDEN.index(k) + 1)
                nc.gpsimd.tensor_tensor(hT[:, LO, k, :], h_f[:, k % 2, :], f(hT[:, HI, k, :]),
                                        ALU.subtract).then_inc(h_lo, 1)

            def prob_low(i, k):
                hf, t = divmod(k, NT)
                eng.wait_ge(e_done, 8 * i + k + 1)
                nc.gpsimd.tensor_tensor(pT[:, LO, hf, :, t * P:(t + 1) * P],
                                        e_f[:, k % 2, :].rearrange("p (c t) -> p c t", t=P),
                                        f(pT[:, HI, hf, :, t * P:(t + 1) * P]), ALU.subtract).then_inc(p_lo_pool, 1)

            def x2_plus_bias(i):
                eng.wait_ge(x2_done, 2 * (i + 1))
                plus_row(x2b, x2, b2_bc).then_inc(x2b_done, 1)

            def weight_low(k):
                raw, high, low, _ = pieces[k]
                eng.wait_ge(w_hi, 2 + k + 1)
                nc.gpsimd.tensor_tensor(low, raw, f(high), ALU.subtract).then_inc(w_lo_pool, 1)

            def step(i, ffn, more, stored):
                for k in range(UNITS):
                    if ffn:
                        hidden_low(i - 1, k)
                    if k in pool_units(i):
                        prob_low(i, k)
                if ffn:
                    if stored:
                        eng.wait_ge(out_stored, 32 * (i - 1))
                    x2_plus_bias(i - 1)
                if more:
                    eng.wait_ge(score_ps, 8 * (i + 1))
                    keys(i + 1)
                    if not ffn:
                        for k in range(len(pieces)):
                            weight_low(k)
                    eng.wait_ge(pv_ps, 4 * (i + 1))
                    values(i + 1)
                    eng.wait_ge(x2_done, 2 * (i + 1))
                    eng.wait_ge(xn_done, 4 * (i + 2))
                    plus_row(xb, x_sb, bo_bc).then_inc(xb_done, 1)

            nc.gpsimd.memset(zero_sb[:, :], 0.0)
            nc.gpsimd.memset(ident[:, :], 0.0).then_inc(setup_pool, 1)
            eng.wait_ge(setup_pool, 1)
            nc.gpsimd.affine_select(out=ident[:, :], in_=ident[:, :], compare_op=ALU.not_equal, fill=1.0,
                                    base=0, pattern=[[-1, P]], channel_multiplier=1).then_inc(setup_pool, 1)
            nc.gpsimd.memset(sel[:, SROW:PW], 0.0)
            eng.wait_ge(setup_pool, 2)
            nc.gpsimd.tensor_copy(sel[:, 0:SROW].rearrange("k (h j) -> k h j", j=KEYS),
                                  ident[0:KEYS, 0:KEYS].unsqueeze(1).broadcast_to([KEYS, HH, KEYS])).then_inc(setup_pool, 1)
            eng.wait_ge(wk_loaded, 32)
            nc.gpsimd.tensor_copy(wk_rep[:, :, :, :],
                                  wk_raw[:, :, :].unsqueeze(2).broadcast_to([P, KC, HH, DH])).then_inc(wk_repeated, 1)
            nc.gpsimd.memset(p_mask[:, :], 1.0)
            nc.gpsimd.memset(v_mask[:, :, :, :], 1.0).then_inc(setup_pool, 1)
            eng.wait_ge(setup_pool, 4)
            nc.gpsimd.affine_select(out=p_mask[:, :], in_=p_mask[:, :], compare_op=ALU.is_ge, fill=0.0,
                                    base=0, pattern=[[-DH, HH]], channel_multiplier=1).then_inc(setup_pool, 1)
            row = [[2 * P - GROW, 2], [P, PAIRS], [-KEYS, GH]]
            nc.gpsimd.affine_select(out=v_mask[:, :, :, :], in_=v_mask[:, :, :, :], compare_op=ALU.is_ge, fill=0.0,
                                    base=0, pattern=row, channel_multiplier=1).then_inc(setup_pool, 1)
            eng.wait_ge(setup_pool, 6)
            nc.gpsimd.affine_select(out=p_mask[:, :], in_=p_mask[:, :], compare_op=ALU.is_ge, fill=0.0,
                                    base=DH - 1, pattern=[[DH, HH]], channel_multiplier=-1).then_inc(setup_pool, 1)
            nc.gpsimd.affine_select(out=v_mask[:, :, :, :], in_=v_mask[:, :, :, :], compare_op=ALU.is_ge, fill=0.0,
                                    base=KEYS - 1, pattern=[[-s, n] for s, n in row],
                                    channel_multiplier=-1).then_inc(setup_pool, 1)
            eng.wait_ge(setup_pool, 8)
            nc.gpsimd.tensor_tensor(k_mask[:, :], p_mask[:, 0:GH], p_mask[:, GH:HH], ALU.add).then_inc(setup_pool, 1)
            for gg in range(2):
                _, den = group_part(gg)
                for a in (HI, LO):
                    dst = v_cur[:, gg, :, a, den].rearrange("p j (h d) -> p j h d", d=DH)
                    mask = v_mask[:, gg, :, :].unsqueeze(3).broadcast_to([P, PAIRS, GH, DH])
                    nc.gpsimd.tensor_scalar(dst, mask, 1.0 if a == HI else 0.0, 0.0, ALU.mult, ALU.add)
            eng.wait_ge(setup_pool, 9)
            eng.wait_ge(setup_dve, 2)
            keys(0)
            eng.wait_ge(bias_loaded, 32)
            eng.wait_ge(x_half_loaded, 16)
            eng.wait_ge(x_loaded, 16)
            plus_row(xb, x_sb, bo_bc).then_inc(xb_done, 1)
            eng.wait_ge(w_hi, 2)
            nc.gpsimd.tensor_tensor(wo[:, LO, :, :], wo_raw[:, :, :], f(wo[:, HI, :, :]),
                                    ALU.subtract).then_inc(w_lo_pool, 1)
            eng.wait_ge(v_rows_made, 1)
            values(0)

            step(0, False, True, False)
            eng.wait_ge(ffn_bias_loaded, 32)
            step(1, True, True, False)
            with eng.Fori(2, NBLK - 1) as i:
                step(i, True, True, True)
            step(NBLK - 1, True, False, True)
            eng.wait_ge(out_stored, 32 * (NBLK - 1))
            x2_plus_bias(NBLK - 1)


_INS = ["x", "ctx_1024", "L0_xattn_Wq", "L0_xattn_bq", "L0_xattn_Wk", "L0_xattn_bk", "L0_xattn_Wv",
        "L0_xattn_bv", "L0_xattn_Wo", "L0_xattn_bo", "L0_ffn_W1", "L0_ffn_b1", "L0_ffn_W2", "L0_ffn_b2"]


def kernel(**inputs):
    import numpy as _np
    import concourse.bacc as _bacc
    from concourse import mybir as _mybir
    from concourse.bass_utils import run_bass_kernel_spmd as _run

    nc = _bacc.Bacc("TRN2", target_bir_lowering=False, num_devices=1)
    arrays, args = {}, []
    for name in _INS:
        a = _np.ascontiguousarray(inputs[name])
        arrays[f"in_{name}_dram"] = a
        args.append(nc.dram_tensor(f"in_{name}_dram", a.shape, _mybir.dt.from_np(a.dtype), kind="ExternalInput").ap())
    out = nc.dram_tensor("out_dram", (NB, SEQ, D), F32, kind="ExternalOutput").ap()
    xattn_ffn(nc, *args, out)
    r = _run(nc, [arrays], core_ids=[0])
    return r.results[0]["out_dram"]
```
